# Optimizing a Trainium2 kernel written in Bass

```python
import numpy as np
import jax
import jax.numpy as jnp

def _softmax(x, axis=-1):
    return jax.nn.softmax(x, axis=axis)

def _gelu(x):
    return jax.nn.gelu(x, approximate=True)

def _silu(x):
    return jax.nn.silu(x)

def _sigmoid(x):
    return jax.nn.sigmoid(x)

def _layernorm(x, axis=-1, eps=1e-05):
    m = jnp.mean(x, axis=axis, keepdims=True)
    v = jnp.var(x, axis=axis, keepdims=True)
    return (x - m) / jnp.sqrt(v + eps)

def _scatter_add(tgt, idx, src, axis=0):
    return tgt.at[idx].add(src)

def _segment_sum(src, seg, n):
    return jax.ops.segment_sum(src, seg, n)
kernel_name = 'mk_flamingo_gated_d1_seqx_r8_c419df'

def setup_inputs(seed: int=0):
    np.random.seed(seed)
    _w = jnp.asarray

    def _rec_inputs():
        import jax
        import jax.numpy as jnp
        _rk = jax.random.key(seed)
        x = -0.0002928 + 1 * jax.random.normal(jax.random.fold_in(_rk, 1), (8, 256, 128), jnp.float32)
        _lenS = 256 - jax.random.randint(jax.random.fold_in(_rk, 7), (8,), 0, max(1, 256 // 4) + 1, jnp.int32)
        _lenS2 = 512 - jax.random.randint(jax.random.fold_in(_rk, 8), (8,), 0, max(1, 512 // 4) + 1, jnp.int32)
        _ctx_1024P = jax.random.normal(jax.random.fold_in(_rk, 11), (8, 16, 128), jnp.float32)
        _ctx_1024c = jax.random.dirichlet(jax.random.fold_in(_rk, 511), 0.3 * jnp.ones((16,), jnp.float32), (8, 512))
        _ctx_1024t = jnp.einsum('bsk,bkd->bsd', _ctx_1024c, _ctx_1024P)
        _ctx_1024t = _ctx_1024t * jax.lax.rsqrt(jnp.mean(jnp.square(_ctx_1024t)) + 1e-12) * 0.953939
        ctx_1024 = 4.13588e-05 + 0.999923 * (_ctx_1024t + 0.3 * jax.random.normal(jax.random.fold_in(_rk, 611), (8, 512, 128), jnp.float32))
        _g = jax.random.normal(jax.random.fold_in(_rk, 9001), (2, 1), jnp.float32)
        _g = jnp.sign(_g) * jnp.maximum(jnp.abs(_g), 1.0) + (_g == 0) * 1.0
        g_xattn = _g[0]
        g_ffn = _g[1]
        return (x, ctx_1024, g_xattn, g_ffn)
    x, ctx_1024, g_xattn, g_ffn = _rec_inputs()

    def _L0_xattn_setup():
        import jax, jax.numpy as jnp
        import numpy as np
        DIM = 128
        NUM_HEADS = 16
        DIM_HEAD = 64
        INNER = NUM_HEADS * DIM_HEAD
        SCALE = DIM_HEAD ** (-0.5)

        def _layernorm(x, gamma, beta, eps=1e-05):
            mu = jnp.mean(x, axis=-1, keepdims=True)
            var = jnp.mean(jnp.square(x - mu), axis=-1, keepdims=True)
            return (x - mu) * jax.lax.rsqrt(var + eps) * gamma + beta
        key = jax.random.key(seed)
        ks = jax.random.split(key, 8)
        B, SQ, SK = (2, 256, 512)
        x = jax.random.normal(ks[0], (B, SQ, DIM), dtype=jnp.float32)
        context = jax.random.normal(ks[1], (B, SK, DIM), dtype=jnp.float32)
        ln_gamma = jnp.ones((DIM,), jnp.float32)
        ln_beta = jnp.zeros((DIM,), jnp.float32)
        w_q = jax.random.normal(ks[2], (DIM, INNER), dtype=jnp.float32) / np.sqrt(DIM)
        w_kv = jax.random.normal(ks[3], (DIM, 2 * INNER), dtype=jnp.float32) / np.sqrt(DIM)
        w_out = jax.random.normal(ks[4], (INNER, DIM), dtype=jnp.float32) / np.sqrt(INNER)
        b_out = jnp.zeros((DIM,), jnp.float32)
        gate = jnp.array([0.5], jnp.float32)
        return {'x': x, 'context': context, 'ln_gamma': ln_gamma, 'ln_beta': ln_beta, 'w_q': w_q, 'w_kv': w_kv, 'w_out': w_out, 'b_out': b_out, 'gate': gate}
    _L0_xattn_all = _L0_xattn_setup()
    _L0_xattn_in = {k: v for k, v in _L0_xattn_all.items() if k in ('ln_gamma', 'ln_beta', 'w_q', 'w_kv', 'w_out', 'b_out', 'gate')}
    del _L0_xattn_all

    def _L0_ffn_setup():
        import jax, jax.numpy as jnp
        import numpy as np
        B, S, D = (4, 256, 128)
        E = 8
        F = 512
        T = B * S
        CAP = 160
        key = jax.random.key(seed)
        k1, k2, k3, k4 = jax.random.split(key, 4)
        inputs = jax.random.normal(k1, (B, S, D), dtype=jnp.float32)
        gate_w = jax.random.normal(k2, (D, E), dtype=jnp.float32) / np.sqrt(D)
        w1 = jax.random.normal(k3, (E, D, F), dtype=jnp.float32) / np.sqrt(D)
        w2 = jax.random.normal(k4, (E, F, D), dtype=jnp.float32) / np.sqrt(F)
        return {'inputs': inputs, 'gate_w': gate_w, 'w1': w1, 'w2': w2}
    _L0_ffn_all = _L0_ffn_setup()
    _L0_ffn_in = {k: v for k, v in _L0_ffn_all.items() if k in ('gate_w', 'w1', 'w2')}
    del _L0_ffn_all
    return {'x': x, 'ctx_1024': ctx_1024, 'g_xattn': g_xattn, 'g_ffn': g_ffn, 'L0_xattn_ln_gamma': _L0_xattn_in['ln_gamma'], 'L0_xattn_ln_beta': _L0_xattn_in['ln_beta'], 'L0_xattn_w_q': _L0_xattn_in['w_q'], 'L0_xattn_w_kv': _L0_xattn_in['w_kv'], 'L0_xattn_w_out': _L0_xattn_in['w_out'], 'L0_xattn_b_out': _L0_xattn_in['b_out'], 'L0_xattn_gate': _L0_xattn_in['gate'], 'L0_ffn_gate_w': _L0_ffn_in['gate_w'], 'L0_ffn_w1': _L0_ffn_in['w1'], 'L0_ffn_w2': _L0_ffn_in['w2']}

def reference(x, ctx_1024, g_xattn, g_ffn, L0_xattn_ln_gamma, L0_xattn_ln_beta, L0_xattn_w_q, L0_xattn_w_kv, L0_xattn_w_out, L0_xattn_b_out, L0_xattn_gate, L0_ffn_gate_w, L0_ffn_w1, L0_ffn_w2):
    import jax
    import jax.numpy as jnp

    def _L0_xattn_ref(x, context, ln_gamma, ln_beta, w_q, w_kv, w_out, b_out, gate):
        import jax, jax.numpy as jnp
        import numpy as np
        DIM = 128
        NUM_HEADS = 16
        DIM_HEAD = 64
        INNER = NUM_HEADS * DIM_HEAD
        SCALE = DIM_HEAD ** (-0.5)

        def _layernorm(x, gamma, beta, eps=1e-05):
            mu = jnp.mean(x, axis=-1, keepdims=True)
            var = jnp.mean(jnp.square(x - mu), axis=-1, keepdims=True)
            return (x - mu) * jax.lax.rsqrt(var + eps) * gamma + beta
        B, SQ, _ = x.shape
        SK = context.shape[1]
        xn = _layernorm(x, ln_gamma, ln_beta)
        q = (xn @ w_q).reshape(B, SQ, NUM_HEADS, DIM_HEAD)
        kv = context @ w_kv
        k, v = jnp.split(kv, 2, axis=-1)
        k = k.reshape(B, SK, NUM_HEADS, DIM_HEAD)
        v = v.reshape(B, SK, NUM_HEADS, DIM_HEAD)
        scores = jnp.einsum('bqhd,bkhd->bhqk', q * SCALE, k)
        attn = jax.nn.softmax(scores, axis=-1)
        out = jnp.einsum('bhqk,bkhd->bqhd', attn, v).reshape(B, SQ, INNER)
        out = out @ w_out + b_out
        return out * jnp.tanh(gate[0])

    def _L0_ffn_ref(inputs, gate_w, w1, w2):
        import jax, jax.numpy as jnp
        import numpy as np
        B, S, D = (4, 256, 128)
        E = 8
        F = 512
        T = B * S
        CAP = 160
        tokens = inputs.reshape(-1, D)
        logits = tokens @ gate_w
        probs = jax.nn.softmax(logits, axis=-1)
        expert_idx = jnp.argmax(probs, axis=-1)
        mask1 = jax.nn.one_hot(expert_idx, E, dtype=tokens.dtype)
        pos = (jnp.cumsum(mask1, axis=0) - 1.0).astype(jnp.int32)
        sec_mask = mask1[:, :, None] * jax.nn.one_hot(pos, CAP, dtype=tokens.dtype)
        combine_weights = probs[:, :, None] * sec_mask
        expert_input = jnp.einsum('tec,td->ecd', sec_mask, tokens)
        h = jax.nn.relu(jnp.einsum('ecd,edf->ecf', expert_input, w1))
        expert_output = jnp.einsum('ecf,efd->ecd', h, w2)
        out = jnp.einsum('tec,ecd->td', combine_weights, expert_output)
        return out.reshape(inputs.shape)
    x = x + jnp.tanh(g_xattn[0]) * _L0_xattn_ref(_layernorm(x, axis=-1), ctx_1024, L0_xattn_ln_gamma, L0_xattn_ln_beta, L0_xattn_w_q, L0_xattn_w_kv, L0_xattn_w_out, L0_xattn_b_out, L0_xattn_gate)
    x = x + jnp.tanh(g_ffn[0]) * _L0_ffn_ref(_layernorm(x, axis=-1), L0_ffn_gate_w, L0_ffn_w1, L0_ffn_w2)
    return x

_drawn_inputs = setup_inputs


def setup_inputs(seed=0):
    import zlib

    import numpy as np

    out = dict(_drawn_inputs(seed))
    spreads = {'L0_xattn_ln_gamma': (1.0, 0.2),
     'L0_xattn_ln_beta': (0.0, 0.449),
     'L0_xattn_b_out': (0.0, 0.1)}
    factors = {}
    for name, (base, spread) in spreads.items():
        noise = np.random.default_rng([zlib.crc32(name.encode()), seed]).standard_normal(out[name].shape)
        drawn = base * np.exp(spread * noise) if base else spread * noise
        out[name] = jnp.asarray(drawn.astype(out[name].dtype))
    for name, factor in factors.items():
        out[name] = (out[name] * factor).astype(out[name].dtype)
    return out
```

```python
from contextlib import ExitStack

import concourse.bass as bass
from concourse import mybir

F32 = mybir.dt.float32
F32R = mybir.dt.float32r
F16 = mybir.dt.float16
BF16 = mybir.dt.bfloat16
U32 = mybir.dt.uint32
ALU = mybir.AluOpType
ACT = mybir.ActivationFunctionType
AX = mybir.AxisListType

P = 128


def gated_block(nc, x, ctx_1024, g_xattn, g_ffn, ln_gamma, ln_beta, w_q, w_kv, w_out, b_out, gate,
                gate_w, w1, w2, out):
    B, SQ, D = x.shape
    SK = ctx_1024.shape[1]
    INNER = w_q.shape[1]
    DH = 64
    H = INNER // DH
    PAIRS = H // 2
    QT = SQ // P
    KT = SK // P
    TT = B * QT
    E, _, F = w1.shape
    FT = F // P
    CAP = 160
    SLOTS = E * CAP
    ST_TILES = SLOTS // P
    SCALE = float(DH) ** -0.5
    EPS = 1e-5
    KQ = SK + SQ
    BK = KQ
    BQ = KQ + SK
    STW = 2 * KQ
    LIFT = 0.875
    BUFS = 4
    DROPPED = 4096.0

    xe_dram = nc.dram_tensor("expert_rows_in", (SLOTS, D), F32).ap()
    ye_dram = nc.dram_tensor("expert_rows_out", (SLOTS, D), F32).ap()

    with ExitStack() as ctx:
        def sb(name, shape, dt):
            return ctx.enter_context(nc.sbuf_tensor(name, shape, dt))

        def pb(name, shape, dt=F32):
            return ctx.enter_context(nc.psum_tensor(name, shape, dt))

        def sem(name):
            return ctx.enter_context(nc.semaphore(name))

        ident = sb("ident", [P, P], F32)
        gamma = sb("gamma", [P, 1], F32)
        beta = sb("beta", [P, 1], F32)
        gates = sb("gates", [P, 3], F32)
        tgates = sb("tgates", [P, 3], F32)
        gscale = sb("gscale", [P, 1], F32)
        w_hi = sb("w_hi", [P, 3 * INNER], F32R)
        w_lo = sb("w_lo", [P, 3 * INNER], F32R)
        wo = sb("wo", [P, PAIRS, D], F32)
        bo = sb("bo", [1, D], F32)
        ones1 = sb("ones1", [1, P], F32)
        X1 = sb("X1", [P, TT, D], F32)
        ctx_raw = sb("ctx_raw", [P, KT, D], F32)
        cT_hi = sb("cT_hi", [P, SK], F32R)
        cT_lo = sb("cT_lo", [P, SK], F32R)
        HI = sb("HI", [P, 2, KQ], F32R)
        LO = sb("LO", [P, 2, KQ], F32R)
        ST = sb("ST", [P, BUFS, 2, STW], F32R)
        VH = sb("VH", [P, KT, H, DH + 2], F16)
        VL = sb("VL", [P, KT, H, DH], F16)
        P32 = sb("P32", [P, 2, KT * SQ], F32)
        PARTS = sb("PARTS", [P, 2, 2, 2, KT * SQ], F16)
        PHI, PLO = PARTS[:, 0], PARTS[:, 1]
        parts32 = PARTS[:].rearrange("p a b h n -> p (a b h n)").bitcast(F32)
        wraw = parts32[:, 0:3 * INNER]
        MX = sb("MX", [P, 2, 2 * QT], F32)
        MROW = sb("MROW", [2 * QT, 2, 2, P], F32R)
        rden = sb("rden", [P, 2, 2 * QT], F32)
        O = sb("O", [P, QT, INNER], F32)
        OT = sb("OT", [P, QT * PAIRS, P], F32)
        stats = sb("stats", [P, TT, 6], F32)
        mv = sb("mv", [P, TT, 2], F32)
        vv = sb("vv", [P, TT], F32)
        rstd = sb("rstd", [P, TT], F32)
        mhalf = sb("mhalf", [P, TT], F32)
        gw = sb("gw", [P, E], F32)
        logit = sb("logit", [P, TT, E], F32)
        lmax = sb("lmax", [P, TT], F32)
        lexp = sb("lexp", [P, TT, E], F32)
        prob = sb("prob", [P, TT], F32)
        cand = sb("cand", [P, TT, E], F32)
        iota_e = sb("iota_e", [P, TT, E], F32)
        first = sb("first", [P, TT], F32)
        hot_padded = sb("hot_padded", [P, 2 * TT, E], BF16)
        hot = hot_padded[:, TT:2 * TT, :]
        tri = sb("tri", [P, P], BF16)
        ones_bf = sb("ones_bf", [P, P], BF16)
        pose = sb("pose", [P, TT, E], F32)
        pos = sb("pos", [P, TT], F32)
        slotf = sb("slotf", [P, TT], F32)
        slot = sb("slot", [P, TT], U32)
        w1s = sb("w1s", [P, E, F], F32)
        with ExitStack() as early:
            xT_hi = early.enter_context(nc.sbuf_tensor("xT_hi", [P, TT * P], F32R))
            xT_lo = early.enter_context(nc.sbuf_tensor("xT_lo", [P, TT * P], F32R))
        w2s = sb("w2s", [P, E, FT, D], F32)
        tok = OT
        p32 = P32[:].rearrange("p h n -> p (h n)")
        tT = p32
        fetched = parts32[:, 0:TT * D].rearrange("p (t d) -> p t d", d=D)
        xe = parts32[:, TT * D:TT * D + SLOTS].rearrange("p (t d) -> p t d", d=D)
        xeT = O[:].rearrange("p q n -> p (q n)")[:, 0:SLOTS]
        hT = VL[:].rearrange("p k h d -> p (k h d)").bitcast(F32)[:, 0:2 * FT * CAP]\
            .rearrange("p (b f c) -> p b f c", b=2, f=FT)
        yT = VH[:].rearrange("p k h d -> p (k h d)").bitcast(F32)[:, 0:SLOTS]
        yrows = p32[:, 0:SLOTS].rearrange("p (t d) -> p t d", d=D)
        zeros = O[:].rearrange("p q n -> p (q n)")

        psS = [pb(f"psS{i}", [P, 512]) for i in range(2)]
        psM = pb("psM", [P, QT, 512])
        psKQ = pb("psKQ", [P, 1024])
        psO = pb("psO", [P, 512])
        psX = pb("psX", [P, 512])

        x_in = sem("x_in")
        small_in = sem("small_in")
        w_in = sem("w_in")
        wo_in = sem("wo_in")
        ctx_in = sem("ctx_in")
        exp_w_in = sem("exp_w_in")
        w2_in = sem("w2_in")
        ident_zero = sem("ident_zero")
        ident_ready = sem("ident_ready")
        pool_consts = sem("pool_consts")
        stack_consts = sem("stack_consts")
        stats_done = sem("stats_done")
        mv_done = sem("mv_done")
        vv_done = sem("vv_done")
        rstd_done = sem("rstd_done")
        xn_done = sem("xn_done")
        w_hi_done = sem("w_hi_done")
        w_lo_done = sem("w_lo_done")
        xt_psum = sem("xt_psum")
        xt_f32 = sem("xt_f32")
        xt_hi_done = sem("xt_hi_done")
        xt_lo_done = sem("xt_lo_done")
        ctxt_psum = sem("ctxt_psum")
        ctxt_hi_done = sem("ctxt_hi_done")
        ctxt_lo_done = sem("ctxt_lo_done")
        kq_psum = sem("kq_psum")
        kq_hi_done = sem("kq_hi_done")
        kq_lo_done = sem("kq_lo_done")
        stack_in = [sem(f"stack_in{i}") for i in range(BUFS)]
        smax_psum = sem("smax_psum")
        max_done = sem("max_done")
        mt_psum = sem("mt_psum")
        mrow_hi_done = sem("mrow_hi_done")
        mrow_lo_done = sem("mrow_lo_done")
        mrow_in = [sem(f"mrow_in{i}") for i in range(2)]
        score_psum = sem("score_psum")
        exp_done = sem("exp_done")
        phi0_done = sem("phi0_done")
        phi1_done = sem("phi1_done")
        plo_done = sem("plo_done")
        v_psum = sem("v_psum")
        v_hi_done = sem("v_hi_done")
        v_lo_done = sem("v_lo_done")
        pv_done = sem("pv_done")
        rden_done = sem("rden_done")
        norm_done = sem("norm_done")
        ot_psum = sem("ot_psum")
        ot_done = sem("ot_done")
        proj_psum = sem("proj_psum")
        x1_done = sem("x1_done")
        tgate_done = sem("tgate_done")
        gscale_done = sem("gscale_done")
        zeros_done = sem("zeros_done")
        zeros_out = sem("zeros_out")
        tok_done = sem("tok_done")
        tokt_psum = sem("tokt_psum")
        tokt_done = sem("tokt_done")
        logit_psum = sem("logit_psum")
        route = sem("route")
        lexp_done = sem("lexp_done")
        pos_psum = sem("pos_psum")
        slot_done = sem("slot_done")
        scattered = sem("scattered")
        xe_in = sem("xe_in")
        xet_psum = sem("xet_psum")
        xet_done = sem("xet_done")
        h_psum = sem("h_psum")
        h_done = sem("h_done")
        y_psum = sem("y_psum")
        y_done = sem("y_done")
        yrow_psum = sem("yrow_psum")
        yrow_done = sem("yrow_done")
        ye_out = sem("ye_out")
        fetch_zero = sem("fetch_zero")
        gathered = sem("gathered")
        final_done = sem("final_done")
        out_done = sem("out_done")

        x_t = x.rearrange("b (t p) d -> p (b t) d", p=P)
        out_t = out.rearrange("b (t p) d -> p (b t) d", p=P)
        ctx_t = ctx_1024.rearrange("b (t p) d -> b p t d", p=P)

        def slots(b):
            for hp in range(PAIRS):
                yield b * PAIRS + hp, hp

        def is_last(b):
            return isinstance(b, int) and b == B - 1

        def is_first(b):
            return isinstance(b, int) and b == 0

        def each_batch(eng, body):
            body(0)
            with eng.Fori(1, B - 1) as b:
                body(b)
            body(B - 1)

        def stack_value(b, hp):
            return b * (160 * PAIRS // BUFS) + 160 * (hp // BUFS + 1)

        def mrow_value(b, hp):
            return b * (64 * PAIRS // 2) + 64 * (hp // 2 + 1)

        def next_pair(b, hp, k):
            return (b, hp + k) if hp + k < PAIRS else (b + 1, hp + k - PAIRS)

        block = ctx.enter_context(nc.Block())

        @block.sync
        def _(sp):
            sp.dma_start(X1[:], x_t).then_inc(x_in, 16)
            sp.dma_start(ctx_raw[:], ctx_t[0]).then_inc(ctx_in, 16)
            sp.dma_start(wraw[:, 0:INNER], w_q).then_inc(w_in, 16)
            sp.dma_start(wraw[:, INNER:3 * INNER], w_kv).then_inc(w_in, 16)
            sp.dma_start(gamma[:], ln_gamma.rearrange("(p o) -> p o", o=1)).then_inc(small_in, 16)
            sp.dma_start(beta[:], ln_beta.rearrange("(p o) -> p o", o=1)).then_inc(small_in, 16)
            for i, g in enumerate((g_xattn, gate, g_ffn)):
                sp.dma_start(gates[:, i:i + 1], g.rearrange("(o n) -> o n", o=1).to_broadcast([P, 1])).then_inc(small_in, 16)
            sp.dma_start(bo[:], b_out.rearrange("(o n) -> o n", o=1)).then_inc(wo_in, 16)
            sp.dma_start(wo[:], w_out.rearrange("(c p) n -> p c n", p=P)).then_inc(wo_in, 16)
            sp.dma_start(gw[:], gate_w).then_inc(exp_w_in, 16)
            sp.dma_start(w1s[:], w1.rearrange("e d f -> d e f")).then_inc(exp_w_in, 16)
            sp.wait_ge(zeros_done, 1)
            sp.dma_start(xe_dram.rearrange("(p t) d -> p (t d)", p=P), zeros[:, 0:SLOTS]).then_inc(zeros_out, 16)

            def stacks(b, hp):
                j = b * PAIRS + hp
                buf, par = hp % BUFS, hp % 2
                sp.wait_ge(kq_lo_done, j + 1)
                sp.wait_ge(kq_hi_done, j + 1)
                if not (is_first(b) and hp < BUFS):
                    sp.wait_ge(score_psum, 4 * j - 4 * (BUFS - 1))
                for h in range(2):
                    src = slice(64 * h, 64 * h + 64)
                    for dst, piece in (
                        (ST[0:64, buf, h, 0:KQ], HI[src, par, :]),
                        (ST[0:64, buf, h, BK:BK + SK], HI[src, par, 0:SK]),
                        (ST[64:128, buf, h, SK:KQ], HI[src, par, SK:KQ]),
                        (ST[64:128, buf, h, 0:SK], LO[src, par, 0:SK]),
                        (ST[0:64, buf, h, BQ:STW], LO[src, par, SK:KQ]),
                    ):
                        sp.dma_start(dst.bitcast(F32), piece.bitcast(F32)).then_inc(stack_in[buf], 16)

            def max_rows(b, hp):
                j = b * PAIRS + hp
                buf, par = hp % BUFS, hp % 2
                sp.wait_ge(mrow_lo_done, j + 1)
                for r in range(2):
                    for h in range(2):
                        dst = ST[64 + r:65 + r, buf, h, BQ:STW].rearrange("o (q c) -> o q c", c=P)
                        sp.dma_start(dst.bitcast(F32), MROW[QT * h:QT * h + QT, par, r, :].bitcast(F32)).then_inc(mrow_in[par], 16)

            sp.wait_ge(stack_consts, 4)
            stacks(0, 0)
            stacks(0, 1)
            max_rows(0, 0)

            def batch(b):
                for j, hp in slots(b):
                    if hp == 0 and not is_last(b):
                        sp.wait_ge(ctxt_psum, b + 1)
                        sp.dma_start(ctx_raw[:], ctx_t[b + 1]).then_inc(ctx_in, 16)
                    if not (is_last(b) and hp + 2 >= PAIRS):
                        stacks(*next_pair(b, hp, 2))
                    if not (is_last(b) and hp + 1 >= PAIRS):
                        max_rows(*next_pair(b, hp, 1))

            each_batch(sp, batch)

            sp.wait_ge(kq_psum, B * PAIRS)
            sp.dma_start(w2s[:], w2.rearrange("e (c p) d -> p e c d", p=P)).then_inc(w2_in, 16)
            sp.wait_ge(scattered, 16 * TT)
            sp.dma_start(xe, xe_dram.rearrange("(t p) d -> p t d", p=P)).then_inc(xe_in, 16)
            sp.wait_ge(yrow_done, 3)
            sp.dma_start(ye_dram.rearrange("(t p) d -> p t d", p=P), yrows).then_inc(ye_out, 16)
            sp.wait_ge(final_done, TT)
            sp.dma_start(out_t, X1[:]).then_inc(out_done, 16)
            sp.wait_ge(out_done, 16)

        @block.gpsimd
        def _(pool):
            pool.memset(ident[:], 0.0).then_inc(ident_zero, 1)
            pool.wait_ge(ident_zero, 1)
            pool.affine_select(out=ident[:], in_=ident[:], compare_op=ALU.not_equal, fill=1.0, base=0,
                               pattern=[[-1, P]], channel_multiplier=1).then_inc(ident_ready, 1)
            pool.memset(mhalf[:], -0.5).then_inc(pool_consts, 1)
            pool.memset(ones1[:], 1.0).then_inc(pool_consts, 1)
            pool.wait_ge(vv_done, 1)
            pool.wait_ge(pool_consts, 1)
            pool.tensor_tensor(rstd[:], vv[:], mhalf[:], ALU.pow).then_inc(rstd_done, 1)
            pool.memset(zeros[:, 0:SLOTS], 0.0).then_inc(zeros_done, 1)
            pool.memset(ones_bf[:], 1.0).then_inc(ident_zero, 1)
            pool.wait_ge(ident_zero, 2)
            pool.affine_select(out=tri[:], in_=ones_bf[:], compare_op=ALU.is_ge, fill=0.0, base=0,
                               pattern=[[1, P]], channel_multiplier=-1).then_inc(pool_consts, 1)
            pool.iota(iota_e[:], pattern=[[0, TT], [1, E]], base=-E, channel_multiplier=0,
                      allow_small_or_imprecise_dtypes=True).then_inc(ident_zero, 1)

            def batch(b):
                for j, hp in slots(b):
                    for h in range(2):
                        par = hp % 2
                        pool.wait_ge(exp_done, 4 * j + 2 * h + 2)
                        pool.wait_ge(phi0_done if h == 0 else phi1_done, j + 1)
                        if not (is_first(b) and hp < 2):
                            pool.wait_ge(pv_done, 2 * j - 4 + h + 1)
                        pool.tensor_tensor(PLO[:, par, h, :], P32[:, h, :], PHI[:, par, h, :],
                                           ALU.subtract).then_inc(plo_done, 1)

            each_batch(pool, batch)

            pool.wait_ge(plo_done, 2 * B * PAIRS)
            pool.wait_ge(pv_done, 2 * B * PAIRS)
            pool.memset(fetched, 0.0).then_inc(fetch_zero, 1)
            pool.wait_ge(vv_done, 2)
            pool.tensor_tensor(rstd[:], vv[:], mhalf[:], ALU.pow).then_inc(rstd_done, 1)
            pool.wait_ge(slot_done, 1)
            pool.wait_ge(zeros_out, 16)
            for t in range(TT):
                pool.indirect_dma_start(out=xe_dram, out_offset=bass.IndirectOffsetOnAxis(slot[:, t:t + 1], 0),
                                        in_=tok[:, t, :], in_offset=None, bounds_check=SLOTS - 1,
                                        oob_is_err=False).then_inc(scattered, 16)
            pool.wait_ge(ye_out, 16)
            pool.wait_ge(fetch_zero, 1)
            for t in range(TT):
                pool.indirect_dma_start(out=fetched[:, t, :], out_offset=None, in_=ye_dram,
                                        in_offset=bass.IndirectOffsetOnAxis(slot[:, t:t + 1], 0),
                                        bounds_check=SLOTS - 1, oob_is_err=False).then_inc(gathered, 16)

        @block.scalar
        def _(act):
            act.wait_ge(small_in, 80)
            act.activation(tgates[:], gates[:], ACT.Tanh).then_inc(tgate_done, 1)
            act.wait_ge(w_in, 32)
            for c in range(3):
                cs = slice(c * INNER, (c + 1) * INNER)
                act.activation(w_hi[:, cs], wraw[:, cs], ACT.Copy).then_inc(w_hi_done, 1)
            for i in range(TT // 4):
                cs = slice(512 * i, 512 * i + 512)
                act.wait_ge(xt_psum, i + 1)
                if i:
                    act.wait_ge(xt_lo_done, i)
                act.activation(P32[:, 0, 0:512], psX[:], ACT.Identity, bias=beta[:, 0:1],
                               scale=gamma[:, 0:1]).then_inc(xt_f32, 1)
                act.wait_ge(xt_f32, i + 1)
                act.activation(xT_hi[:, cs], P32[:, 0, 0:512], ACT.Copy).then_inc(xt_hi_done, 1)

            def ctxt_hi(b):
                act.wait_ge(ctxt_psum, b + 1)
                act.activation(cT_hi[:], psX[:], ACT.Copy).then_inc(ctxt_hi_done, 1)

            def kq_hi(b, hp):
                j = b * PAIRS + hp
                act.wait_ge(kq_psum, j + 1)
                if not (is_first(b) and hp < 2):
                    pb_, php = (b, hp - 2) if hp >= 2 else (b - 1, hp - 2 + PAIRS)
                    act.wait_ge(stack_in[php % BUFS], stack_value(pb_, php))
                act.activation(HI[:, hp % 2, :], psKQ[:, 0:KQ], ACT.Copy).then_inc(kq_hi_done, 1)

            def v_hi(b, half, kt):
                n = b * 2 * KT + half * KT + kt
                act.wait_ge(v_psum, n + 1)
                act.activation(VH[:, kt, 8 * half:8 * half + 8, 0:DH],
                               psX[:].rearrange("p (h d) -> p h d", d=DH), ACT.Copy).then_inc(v_hi_done, 1)

            def ot_copy(b, i):
                act.wait_ge(ot_psum, b * 4 + i + 1)
                if not (is_first(b)):
                    act.wait_ge(proj_psum, b)
                act.activation(OT[:, 4 * i:4 * i + 4, :], psX[:].rearrange("p (t c) -> p t c", c=P),
                               ACT.Copy).then_inc(ot_done, 1)

            def exps(j, c, first_pairs):
                h = c // 2
                act.wait_ge(score_psum, 4 * j + c + 1)
                if not (first_pairs):
                    act.wait_ge(plo_done, 2 * j - 2 + h + 1)
                act.activation(P32[:, h, 512 * (c % 2):512 * (c % 2) + 512], psS[c % 2][:], ACT.Exp,
                               scale=SCALE).then_inc(exp_done, 1)

            ctxt_hi(0)
            kq_hi(0, 0)
            kq_hi(0, 1)
            for kt in range(KT):
                v_hi(0, 0, kt)
            act.wait_ge(xt_lo_done, TT // 4)

            def batch(b):
                for j, hp in slots(b):
                    start = is_first(b) and hp == 0
                    exps(j, 0, start)
                    exps(j, 1, start)
                    exps(j, 2, start)
                    if not (is_last(b) and hp + 2 >= PAIRS):
                        kq_hi(*next_pair(b, hp, 2))
                    exps(j, 3, start)
                    act.wait_ge(exp_done, 4 * j + 4)
                    if not (is_first(b) and hp < 2):
                        act.wait_ge(pv_done, 2 * j - 2)
                    act.activation(PHI[:, hp % 2, 1, :], P32[:, 1, :], ACT.Copy).then_inc(phi1_done, 1)
                    if hp == 1 and not is_first(b):
                        for i in range(4):
                            ot_copy(b - 1, i)
                    if hp in (3, 4):
                        for kt in (2 * hp - 6, 2 * hp - 5):
                            v_hi(b, 1, kt)
                    if hp == 5 and not is_last(b):
                        ctxt_hi(b + 1)
                    if hp in (6, 7) and not is_last(b):
                        for kt in (2 * hp - 12, 2 * hp - 11):
                            v_hi(b + 1, 0, kt)

            each_batch(act, batch)
            for i in range(4):
                ot_copy(B - 1, i)

            for i in range(TT // 4):
                act.wait_ge(tokt_psum, i + 1)
                act.activation(tT[:, 512 * i:512 * i + 512], psS[i % 2][:], ACT.Copy).then_inc(tokt_done, 1)
            act.wait_ge(route, 2)
            act.activation(lexp[:], cand[:], ACT.Exp).then_inc(lexp_done, 1)
            for i in range(3):
                n = min(4, ST_TILES - 4 * i)
                act.wait_ge(xet_psum, i + 1)
                act.activation(xeT[:, 512 * i:512 * i + n * P], psS[i % 2][:, 0:n * P], ACT.Copy).then_inc(xet_done, 1)
            for e in range(E):
                for i in range(2):
                    act.wait_ge(h_psum, 2 * e + i + 1)
                    if e >= 2:
                        act.wait_ge(y_psum, e - 1)
                    act.activation(hT[:, e % 2, 2 * i:2 * i + 2, :],
                                   psM[:, i, 0:2 * CAP].rearrange("p (f c) -> p f c", f=2), ACT.Relu).then_inc(h_done, 1)

        @block.vector
        def _(dve):
            dve.memset(ST[:].bitcast(F32)[64:128, :, :, BK:BQ], 1.0).then_inc(stack_consts, 1)
            dve.memset(ST[:].bitcast(F32)[64:128, :, :, BQ:STW], LIFT).then_inc(stack_consts, 1)
            dve.memset(VH[:], 1.0).then_inc(stack_consts, 1)
            dve.memset(hot_padded[:, 0:TT, :], 0.0).then_inc(stack_consts, 1)

            def normalise(n, dst):
                for t in range(TT):
                    dve.bn_stats(stats[:, t, :], X1[:, t, :]).then_inc(stats_done, 1)
                for t in range(TT):
                    dve.wait_ge(stats_done, TT * n + t + 1)
                    dve.bn_aggr(mv[:, t, :], stats[:, t, :]).then_inc(mv_done, 1)
                dve.wait_ge(mv_done, TT * n + TT)

            dve.wait_ge(x_in, 16)
            normalise(0, None)
            dve.tensor_scalar(vv[:], mv[:, :, 1], 1.0 + EPS, EPS * EPS, ALU.mult, ALU.add).then_inc(vv_done, 1)
            dve.wait_ge(rstd_done, 1)
            for t in range(TT):
                dve.tensor_scalar(OT[:, t, :], X1[:, t, :], mv[:, t, 0:1], rstd[:, t:t + 1], ALU.subtract,
                                  ALU.mult).then_inc(xn_done, 1)
            for c in range(3):
                cs = slice(c * INNER, (c + 1) * INNER)
                dve.wait_ge(w_hi_done, c + 1)
                dve.tensor_tensor(w_lo[:, cs], wraw[:, cs], w_hi[:, cs].bitcast(F32), ALU.subtract).then_inc(w_lo_done, 1)
            for i in range(TT // 4):
                cs = slice(512 * i, 512 * i + 512)
                dve.wait_ge(xt_hi_done, i + 1)
                dve.tensor_tensor(xT_lo[:, cs], P32[:, 0, 0:512], xT_hi[:, cs].bitcast(F32), ALU.subtract)\
                   .then_inc(xt_lo_done, 1)
            dve.wait_ge(tgate_done, 1)
            dve.tensor_tensor(gscale[:], tgates[:, 0:1], tgates[:, 1:2], ALU.mult).then_inc(gscale_done, 1)

            def ctxt_lo(b):
                dve.wait_ge(ctxt_hi_done, b + 1)
                dve.tensor_tensor(cT_lo[:], psX[:], cT_hi[:].bitcast(F32), ALU.subtract).then_inc(ctxt_lo_done, 1)

            def kq_lo(b, hp):
                j = b * PAIRS + hp
                dve.wait_ge(kq_hi_done, j + 1)
                dve.tensor_tensor(LO[:, hp % 2, :], psKQ[:, 0:KQ], HI[:, hp % 2, :].bitcast(F32), ALU.subtract)\
                   .then_inc(kq_lo_done, 1)

            def v_lo(b, half, kt):
                n = b * 2 * KT + half * KT + kt
                dve.wait_ge(v_hi_done, n + 1)
                dve.tensor_tensor(VL[:, kt, 8 * half:8 * half + 8, :], psX[:].rearrange("p (h d) -> p h d", d=DH),
                                  VH[:, kt, 8 * half:8 * half + 8, 0:DH], ALU.subtract).then_inc(v_lo_done, 1)

            def row_max(b, hp, h):
                j = b * PAIRS + hp
                dve.wait_ge(smax_psum, 2 * j + h + 1)
                if not (is_first(b) and hp < 2):
                    dve.wait_ge(mt_psum, j - 1)
                dve.tensor_reduce(MX[:, hp % 2, QT * h:QT * h + QT], psM[:], AX.X, ALU.max).then_inc(max_done, 1)

            def max_row(b, hp):
                j = b * PAIRS + hp
                par = hp % 2
                dve.wait_ge(mt_psum, j + 1)
                if not (is_first(b) and hp < 2):
                    pb_, php = (b, hp - 2) if hp >= 2 else (b - 1, hp - 2 + PAIRS)
                    dve.wait_ge(mrow_in[par], mrow_value(pb_, php))
                dve.tensor_scalar(MROW[:, par, 0, :], psX[0:2 * QT, 0:P], -1.0, None, ALU.mult).then_inc(mrow_hi_done, 1)
                dve.wait_ge(mrow_hi_done, j + 1)
                dve.scalar_tensor_tensor(out=MROW[:, par, 1, :], in0=psX[0:2 * QT, 0:P], scalar=-1.0,
                                         in1=MROW[:, par, 0, :].bitcast(F32), op0=ALU.mult, op1=ALU.subtract)\
                   .then_inc(mrow_lo_done, 1)

            def normalise_heads(b, hp, start_of_all):
                j = b * PAIRS + hp
                sums = psO[:, 0:2 * QT * (DH + 1)].rearrange("p (g d) -> p g d", d=DH + 1)
                dve.wait_ge(pv_done, 2 * j + 2)
                dve.reciprocal(rden[:, hp % 2, :], sums[:, :, DH]).then_inc(rden_done, 1)
                dve.wait_ge(rden_done, j + 1)
                if hp == 0 and not start_of_all:
                    dve.wait_ge(ot_psum, b * 4)
                if start_of_all:
                    dve.wait_ge(zeros_out, 16)
                o = O[:, :, P * hp:P * hp + P].rearrange("p q (h d) -> p h q d", h=2)
                dve.tensor_tensor(o, sums[:, :, 0:DH].rearrange("p (h q) d -> p h q d", h=2),
                                  rden[:, hp % 2, :].rearrange("p (h q) -> p h q", h=2).unsqueeze(3)
                                  .to_broadcast([P, 2, QT, DH]), ALU.mult).then_inc(norm_done, 1)

            def add_attention(b):
                dve.wait_ge(proj_psum, b + 1)
                xs = X1[:, bass.ds(b * QT, QT), :]
                dve.scalar_tensor_tensor(out=xs, in0=psX[:, 0:QT * D].rearrange("p (q d) -> p q d", q=QT),
                                         scalar=gscale[:, 0:1], in1=xs, op0=ALU.mult, op1=ALU.add).then_inc(x1_done, 1)

            ctxt_lo(0)
            kq_lo(0, 0)
            kq_lo(0, 1)
            for kt in range(KT):
                v_lo(0, 0, kt)
            row_max(0, 0, 0)
            row_max(0, 0, 1)
            max_row(0, 0)
            dve.wait_ge(gscale_done, 1)

            def batch(b):
                for j, hp in slots(b):
                    more1 = not (is_last(b) and hp + 1 >= PAIRS)
                    if more1:
                        row_max(*next_pair(b, hp, 1), 0)
                        row_max(*next_pair(b, hp, 1), 1)
                    dve.wait_ge(exp_done, 4 * j + 2)
                    if not (is_first(b) and hp < 2):
                        dve.wait_ge(pv_done, 2 * j - 3)
                    dve.tensor_copy(PHI[:, hp % 2, 0, :], P32[:, 0, :]).then_inc(phi0_done, 1)
                    if not (is_last(b) and hp + 2 >= PAIRS):
                        kq_lo(*next_pair(b, hp, 2))
                    if more1:
                        max_row(*next_pair(b, hp, 1))
                    if not (is_first(b) and hp == 0):
                        pb_, php = (b, hp - 1) if hp >= 1 else (b - 1, PAIRS - 1)
                        normalise_heads(pb_, php, is_first(b) and hp == 1)
                    if hp == 2 and not is_first(b):
                        add_attention(b - 1)
                    if hp in (3, 4):
                        for kt in (2 * hp - 6, 2 * hp - 5):
                            v_lo(b, 1, kt)
                    if hp == 5 and not is_last(b):
                        ctxt_lo(b + 1)
                    if hp in (6, 7) and not is_last(b):
                        for kt in (2 * hp - 12, 2 * hp - 11):
                            v_lo(b + 1, 0, kt)

            each_batch(dve, batch)
            normalise_heads(B - 1, PAIRS - 1, False)
            add_attention(B - 1)

            dve.wait_ge(x1_done, B)
            normalise(1, None)
            dve.tensor_scalar(vv[:], mv[:, :, 1], EPS, None, ALU.add).then_inc(vv_done, 1)
            dve.wait_ge(rstd_done, 2)
            for t in range(TT):
                dve.tensor_scalar(tok[:, t, :], X1[:, t, :], mv[:, t, 0:1], rstd[:, t:t + 1], ALU.subtract,
                                  ALU.mult).then_inc(tok_done, 1)

            def wide(a):
                return a.unsqueeze(2).to_broadcast([P, TT, E])

            step = [0]

            def then(ins):
                step[0] += 1
                ins.then_inc(route, 1)
                dve.wait_ge(route, step[0])

            lg = psX[:, 0:TT * E].rearrange("p (t e) -> p t e", e=E)
            dve.wait_ge(logit_psum, 1)
            then(dve.tensor_reduce(lmax[:], lg, AX.X, ALU.max))
            then(dve.tensor_tensor(cand[:], lg, wide(lmax[:]), ALU.subtract))
            dve.wait_ge(ident_zero, 3)
            then(dve.scalar_tensor_tensor(out=logit[:], in0=cand[:], scalar=0.0, in1=iota_e[:],
                                          op0=ALU.is_equal, op1=ALU.mult))
            then(dve.tensor_reduce(first[:], logit[:], AX.X, ALU.min))
            then(dve.tensor_tensor(hot, iota_e[:], wide(first[:]), ALU.is_equal))
            dve.wait_ge(lexp_done, 1)
            then(dve.tensor_reduce(lmax[:], lexp[:], AX.X, ALU.add))
            then(dve.reciprocal(prob[:], lmax[:]))
            then(dve.tensor_scalar(prob[:], prob[:], tgates[:, 2:3], None, ALU.mult))
            dve.wait_ge(pos_psum, 1)
            then(dve.tensor_tensor(pose[:], psO[:, 0:TT * E].rearrange("p (t e) -> p t e", e=E), hot, ALU.mult))
            then(dve.tensor_reduce(pos[:], pose[:], AX.X, ALU.add))
            then(dve.tensor_scalar(slotf[:], first[:], float(CAP), float(E * CAP - 1), ALU.mult, ALU.add))
            then(dve.tensor_tensor(slotf[:], slotf[:], pos[:], ALU.add))
            then(dve.tensor_scalar(pos[:], pos[:], float(CAP), DROPPED, ALU.is_gt, ALU.mult))
            dve.tensor_tensor(slot[:], slotf[:], pos[:], ALU.add).then_inc(slot_done, 1)

            for e in range(E):
                dve.wait_ge(y_psum, e + 1)
                dve.tensor_copy(yT[:, e * CAP:(e + 1) * CAP], [psO, psX][e % 2][:, 0:CAP]).then_inc(y_done, 1)
            for i in range(3):
                n = min(4, ST_TILES - 4 * i)
                dve.wait_ge(yrow_psum, i + 1)
                dve.tensor_copy(yrows[:, 4 * i:4 * i + n, :],
                                psS[i % 2][:, 0:n * P].rearrange("p (t d) -> p t d", d=D)).then_inc(yrow_done, 1)
            dve.wait_ge(gathered, 16 * TT)
            for t in range(TT):
                dve.scalar_tensor_tensor(out=X1[:, t, :], in0=fetched[:, t, :], scalar=prob[:, t:t + 1],
                                         in1=X1[:, t, :], op0=ALU.mult, op1=ALU.add).then_inc(final_done, 1)

        @block.tensor
        def _(pe):
            def matmul3(dst, hi_l, lo_l, hi_r, lo_r):
                pe.matmul(dst, hi_l, hi_r, start=True, stop=False)
                pe.matmul(dst, hi_l, lo_r, start=False, stop=False)
                return pe.matmul(dst, lo_l, hi_r, start=False, stop=True)

            x_free = [None]

            def wait_x(free_when):
                if x_free[0]:
                    pe.wait_ge(*x_free[0])
                x_free[0] = free_when

            def ctx_transposes(b):
                pe.wait_ge(ctx_in, 16 * b + 16)
                wait_x((ctxt_lo_done, b + 1))
                for kt in range(KT):
                    last = pe.transpose(psX[:, P * kt:P * kt + P], ctx_raw[:, kt, :], ident[:])
                last.then_inc(ctxt_psum, 1)

            def kq_project(b, hp):
                j = b * PAIRS + hp
                if not (is_first(b) and hp == 0):
                    pe.wait_ge(kq_lo_done, j)
                if hp == 0:
                    pe.wait_ge(ctxt_lo_done, b + 1)
                k_cols = slice(INNER + P * hp, INNER + P * hp + P)
                q_cols = slice(P * hp, P * hp + P)
                xs = bass.ds(b * SQ, SQ)
                matmul3(psKQ[:, 0:SK], w_hi[:, k_cols], w_lo[:, k_cols], cT_hi[:], cT_lo[:])
                matmul3(psKQ[:, SK:KQ], w_hi[:, q_cols], w_lo[:, q_cols], xT_hi[:, xs], xT_lo[:, xs])\
                    .then_inc(kq_psum, 1)

            def v_project(b, half, kt):
                wait_x((v_lo_done, b * 2 * KT + half * KT + kt + 1))
                pe.wait_ge(ctxt_lo_done, b + 1)
                cs = slice(P * kt, P * kt + P)
                ws = slice(2 * INNER + 512 * half, 2 * INNER + 512 * half + 512)
                matmul3(psX[:], cT_hi[:, cs], cT_lo[:, cs], w_hi[:, ws], w_lo[:, ws]).then_inc(v_psum, 1)

            def max_scores(b, hp, h):
                j = b * PAIRS + hp
                buf = hp % BUFS
                if h == 0:
                    pe.wait_ge(stack_in[buf], stack_value(b, hp))
                if not (is_first(b) and hp == 0 and h == 0):
                    pe.wait_ge(max_done, 2 * j + h)
                for qt in range(QT):
                    last = pe.matmul(psM[:, qt, :], ST[:, buf, h, SK + P * qt:SK + P * qt + P],
                                     ST[:, buf, h, 0:SK], start=True, stop=True)
                last.then_inc(smax_psum, 1)

            def max_transpose(b, hp):
                j = b * PAIRS + hp
                pe.wait_ge(max_done, 2 * j + 2)
                wait_x((mrow_lo_done, j + 1))
                pe.transpose(psX[0:2 * QT, 0:P], MX[:, hp % 2, :], ident[:]).then_inc(mt_psum, 1)

            def scores(b, hp, c):
                j = b * PAIRS + hp
                buf, h = hp % BUFS, c // 2
                if c == 0:
                    pe.wait_ge(mrow_in[hp % 2], mrow_value(b, hp))
                if not (is_first(b) and hp == 0 and c < 2):
                    pe.wait_ge(exp_done, 4 * j + c - 1)
                for i in range(2):
                    kt = 2 * (c % 2) + i
                    dst = psS[c % 2][:, SQ * i:SQ * i + SQ]
                    pe.matmul(dst, ST[:, buf, h, P * kt:P * kt + P], ST[:, buf, h, SK:KQ], start=True, stop=False)
                    last = pe.matmul(dst, ST[:, buf, h, BK + P * kt:BK + P * kt + P], ST[:, buf, h, BQ:STW],
                                     start=False, stop=True)
                last.then_inc(score_psum, 1)

            def values(b, hp, h):
                j = b * PAIRS + hp
                par, head = hp % 2, 2 * hp + h
                pe.wait_ge(plo_done, 2 * j + h + 1)
                if h == 0:
                    if not (is_first(b) and hp == 0):
                        pe.wait_ge(norm_done, j)
                    if hp % 4 == 0:
                        pe.wait_ge(v_lo_done, b * 2 * KT + KT * (hp // 4 + 1))
                for qt in range(QT):
                    g = (h * QT + qt) * (DH + 1)
                    for kt in range(KT):
                        cs = slice(SQ * kt + P * qt, SQ * kt + P * qt + P)
                        phi, plo = PHI[:, par, h, cs], PLO[:, par, h, cs]
                        first_, last_ = kt == 0, kt == KT - 1
                        pe.matmul(psO[:, g:g + DH + 1], phi, VH[:, kt, head, 0:DH + 1], start=first_, stop=False)
                        pe.matmul(psO[:, g:g + DH], phi, VL[:, kt, head, :], start=False, stop=False)
                        last = pe.matmul(psO[:, g:g + DH + 1], plo, VH[:, kt, head, 0:DH + 1], start=False,
                                         stop=last_)
                last.then_inc(pv_done, 1)

            def o_transposes(b, i):
                wait_x((ot_done, b * 4 + i + 1))
                if i == 0:
                    pe.wait_ge(norm_done, b * PAIRS + PAIRS)
                for n in range(4):
                    qt, pair = divmod(4 * i + n, PAIRS)
                    last = pe.transpose(psX[:, P * n:P * n + P], O[:, qt, P * pair:P * pair + P], ident[:])
                last.then_inc(ot_psum, 1)

            def project(b):
                wait_x((x1_done, b + 1))
                pe.wait_ge(ot_done, b * 4 + 4)
                for qt in range(QT):
                    dst = psX[:, D * qt:D * qt + D]
                    pe.matmul(dst, ones1[:], bo[:], start=True, stop=False)
                    for pair in range(PAIRS):
                        last = pe.matmul(dst, OT[:, qt * PAIRS + pair, :], wo[:, pair, :], start=False,
                                         stop=(pair == PAIRS - 1))
                last.then_inc(proj_psum, 1)

            pe.wait_ge(ident_ready, 1)
            for i in range(TT // 4):
                wait_x((xt_f32, i + 1))
                for n in range(4):
                    pe.wait_ge(xn_done, 4 * i + n + 1)
                    last = pe.transpose(psX[:, P * n:P * n + P], OT[:, 4 * i + n, :], ident[:])
                last.then_inc(xt_psum, 1)
            ctx_transposes(0)
            pe.wait_ge(w_lo_done, 3)
            pe.wait_ge(xt_lo_done, TT // 4)
            kq_project(0, 0)
            kq_project(0, 1)
            pe.wait_ge(stack_consts, 4)
            for kt in range(KT):
                v_project(0, 0, kt)
            max_scores(0, 0, 0)
            max_scores(0, 0, 1)
            max_transpose(0, 0)
            pe.wait_ge(wo_in, 32)

            def batch(b):
                if not is_first(b):
                    x_free[0] = (v_lo_done, b * 2 * KT + KT)
                for j, hp in slots(b):
                    more1 = not (is_last(b) and hp + 1 >= PAIRS)
                    more2 = not (is_last(b) and hp + 2 >= PAIRS)
                    older = not (is_first(b) and hp == 0)
                    prev = (b, hp - 1) if hp >= 1 else (b - 1, PAIRS - 1)
                    if more1:
                        max_scores(*next_pair(b, hp, 1), 0)
                    scores(b, hp, 0)
                    scores(b, hp, 1)
                    if older:
                        values(*prev, 0)
                    if more1:
                        max_scores(*next_pair(b, hp, 1), 1)
                    scores(b, hp, 2)
                    if more2:
                        kq_project(*next_pair(b, hp, 2))
                    if more1:
                        max_transpose(*next_pair(b, hp, 1))
                    scores(b, hp, 3)
                    if older:
                        values(*prev, 1)
                    if hp == 1 and not is_first(b):
                        for i in range(4):
                            o_transposes(b - 1, i)
                    if hp == 2 and not is_first(b):
                        project(b - 1)
                    if hp in (3, 4):
                        for kt in (2 * hp - 6, 2 * hp - 5):
                            v_project(b, 1, kt)
                    if hp == 5 and not is_last(b):
                        ctx_transposes(b + 1)
                    if hp in (6, 7) and not is_last(b):
                        for kt in (2 * hp - 12, 2 * hp - 11):
                            v_project(b + 1, 0, kt)
                if is_last(b):
                    values(b, PAIRS - 1, 0)
                    values(b, PAIRS - 1, 1)
                    for i in range(4):
                        o_transposes(b, i)
                    project(b)

            each_batch(pe, batch)

            for i in range(TT // 4):
                if i >= 2:
                    pe.wait_ge(tokt_done, i - 1)
                for n in range(4):
                    pe.wait_ge(tok_done, 4 * i + n + 1)
                    last = pe.transpose(psS[i % 2][:, P * n:P * n + P], tok[:, 4 * i + n, :], ident[:])
                last.then_inc(tokt_psum, 1)
            pe.wait_ge(tokt_done, TT // 4)
            pe.wait_ge(exp_w_in, 32)
            for t in range(TT):
                last = pe.matmul(psX[:, E * t:E * t + E], tT[:, P * t:P * t + P], gw[:], start=True, stop=True)
            last.then_inc(logit_psum, 1)
            pe.wait_ge(route, 5)
            pe.wait_ge(pool_consts, 3)
            hots = hot_padded[:].rearrange("p t e -> p (t e)")
            pe.matmul(psO[:, 0:TT * E], tri[:], hots[:, TT * E:2 * TT * E], start=True, stop=False)
            for s in range(1, TT):
                last = pe.matmul(psO[:, 0:TT * E], ones_bf[:], hots[:, (TT - s) * E:(2 * TT - s) * E],
                                 start=False, stop=(s == TT - 1))
            last.then_inc(pos_psum, 1)
            pe.wait_ge(xe_in, 16)
            for i in range(3):
                if i == 2:
                    pe.wait_ge(xet_done, 1)
                for n in range(min(4, ST_TILES - 4 * i)):
                    last = pe.transpose(psS[i % 2][:, P * n:P * n + P], xe[:, 4 * i + n, :], ident[:])
                last.then_inc(xet_psum, 1)
            pe.wait_ge(xet_done, 3)
            pe.wait_ge(w2_in, 16)

            def up(e):
                for i in range(2):
                    if e:
                        pe.wait_ge(h_done, 2 * e - 1 + i)
                    for f in (2 * i, 2 * i + 1):
                        last = pe.matmul(psM[:, i, (f % 2) * CAP:(f % 2) * CAP + CAP], w1s[:, e, P * f:P * f + P],
                                         xeT[:, e * CAP:(e + 1) * CAP], start=True, stop=True)
                    last.then_inc(h_psum, 1)

            def down(e):
                pe.wait_ge(h_done, 2 * e + 2)
                if e >= 2:
                    pe.wait_ge(y_done, e - 1)
                for f in range(FT):
                    last = pe.matmul([psO, psX][e % 2][:, 0:CAP], w2s[:, e, f, :], hT[:, e % 2, f, :],
                                     start=(f == 0), stop=(f == FT - 1))
                last.then_inc(y_psum, 1)

            for e in range(E):
                up(e)
                if e:
                    down(e - 1)
            down(E - 1)
            pe.wait_ge(y_done, E)
            for i in range(3):
                if i == 2:
                    pe.wait_ge(yrow_done, 1)
                for n in range(min(4, ST_TILES - 4 * i)):
                    s = 4 * i + n
                    last = pe.transpose(psS[i % 2][:, P * n:P * n + P], yT[:, P * s:P * s + P], ident[:])
                last.then_inc(yrow_psum, 1)


_INS = ['x', 'ctx_1024', 'g_xattn', 'g_ffn', 'L0_xattn_ln_gamma', 'L0_xattn_ln_beta', 'L0_xattn_w_q',
        'L0_xattn_w_kv', 'L0_xattn_w_out', 'L0_xattn_b_out', 'L0_xattn_gate', 'L0_ffn_gate_w',
        'L0_ffn_w1', 'L0_ffn_w2']
_OUTS = [((8, 256, 128), 'float32')]


def kernel(**inputs):
    import numpy as _np
    import concourse.bacc as _bacc
    from concourse import mybir as _mybir
    from concourse.bass_utils import run_bass_kernel_spmd as _run

    nc = _bacc.Bacc("TRN2", target_bir_lowering=False, num_devices=1)
    arrays, args = {}, {}
    for name in _INS:
        a = _np.ascontiguousarray(inputs[name])
        arrays[f"in_{name}_dram"] = a
        args[name] = nc.dram_tensor(f"in_{name}_dram", a.shape, _mybir.dt.from_np(a.dtype), kind="ExternalInput").ap()
    for i, (shape, dtype) in enumerate(_OUTS):
        dt = _mybir.dt.from_np(_np.dtype(dtype))
        out = nc.dram_tensor(f"out_{i}_dram", shape, dt, kind="ExternalOutput").ap()
    gated_block(nc, args['x'], args['ctx_1024'], args['g_xattn'], args['g_ffn'], args['L0_xattn_ln_gamma'],
                args['L0_xattn_ln_beta'], args['L0_xattn_w_q'], args['L0_xattn_w_kv'], args['L0_xattn_w_out'],
                args['L0_xattn_b_out'], args['L0_xattn_gate'], args['L0_ffn_gate_w'], args['L0_ffn_w1'],
                args['L0_ffn_w2'], out)
    r = _run(nc, [arrays], core_ids=[0])
    return r.results[0]["out_0_dram"]
```

```python
from contextlib import ExitStack

import concourse.bass as bass
from concourse import mybir

F32 = mybir.dt.float32
F32R = mybir.dt.float32r
F16 = mybir.dt.float16
BF16 = mybir.dt.bfloat16
U32 = mybir.dt.uint32
ALU = mybir.AluOpType
ACT = mybir.ActivationFunctionType
AX = mybir.AxisListType

P = 128


def gated_block(nc, x, ctx_1024, g_xattn, g_ffn, ln_gamma, ln_beta, w_q, w_kv, w_out, b_out, gate,
                gate_w, w1, w2, out):
    B, SQ, D = x.shape
    SK = ctx_1024.shape[1]
    INNER = w_q.shape[1]
    DH = 64
    H = INNER // DH
    PAIRS = H // 2
    QT = SQ // P
    KT = SK // P
    TT = B * QT
    E, _, F = w1.shape
    FT = F // P
    CAP = 160
    SLOTS = E * CAP
    ST_TILES = SLOTS // P
    SCALE = float(DH) ** -0.5
    EPS = 1e-5
    KQ = SK + SQ
    BQ, BK, AK, AQ = 0, SQ, KQ, KQ + SK
    STW = 2 * KQ
    H_QLO, H_KHI, H_QHI, H_KLO, H_QHI2 = 0, SQ, SQ + SK, 2 * SQ + SK, 2 * KQ
    HLW = 2 * KQ + SQ
    LIFT = 0.875
    AHEAD = 4
    BUFS = AHEAD
    DROPPED = 4096.0

    xe_dram = nc.dram_tensor("expert_rows_in", (SLOTS, D), F32).ap()
    ye_dram = nc.dram_tensor("expert_rows_out", (SLOTS, D), F32).ap()

    with ExitStack() as ctx:
        def sb(name, shape, dt):
            return ctx.enter_context(nc.sbuf_tensor(name, shape, dt))

        def pb(name, shape, dt=F32):
            return ctx.enter_context(nc.psum_tensor(name, shape, dt))

        def sem(name):
            return ctx.enter_context(nc.semaphore(name))

        ident = sb("ident", [P, P], F32)
        gamma = sb("gamma", [P, 1], F32)
        beta = sb("beta", [P, 1], F32)
        gates = sb("gates", [P, 3], F32)
        tgates = sb("tgates", [P, 3], F32)
        gscale = sb("gscale", [P, 1], F32)
        w_hi = sb("w_hi", [P, 3 * INNER], F32R)
        w_lo = sb("w_lo", [P, 3 * INNER], F32R)
        wo = sb("wo", [P, PAIRS, D], F32)
        bo = sb("bo", [1, D], F32)
        ones1 = sb("ones1", [1, P], F32)
        X1 = sb("X1", [P, TT, D], F32)
        ctx_raw = sb("ctx_raw", [P, KT, D], F32)
        cT_hi = sb("cT_hi", [P, SK], F32R)
        cT_lo = sb("cT_lo", [P, SK], F32R)
        HL = sb("HL", [P, 2, HLW], F32R)
        ST = sb("ST", [P, BUFS, 2, STW], F32R)
        VH = sb("VH", [P, KT, H, DH + 2], F16)
        VL = sb("VL", [P, KT, H, DH], F16)
        P32 = sb("P32", [P, 2, KT * SQ], F32)
        PARTS = sb("PARTS", [P, 2, 2, 2, KT * SQ], F16)
        PHI, PLO = PARTS[:, 0], PARTS[:, 1]
        parts32 = PARTS[:].rearrange("p a b h n -> p (a b h n)").bitcast(F32)
        wraw = parts32[:, 0:3 * INNER]
        MX = sb("MX", [P, 2, 2, QT], F32)
        MXS = sb("MXS", [P, 2, QT, 2, 2], F32R)
        MROW = sb("MROW", [4, 2, SQ], F32R)
        rden = sb("rden", [P, 2, 2 * QT], F32)
        O = sb("O", [P, QT, INNER], F32)
        OT = sb("OT", [P, QT * PAIRS, P], F32)
        stats = sb("stats", [P, TT, 6], F32)
        mv = sb("mv", [P, TT, 2], F32)
        vv = sb("vv", [P, TT], F32)
        rstd = sb("rstd", [P, TT], F32)
        mhalf = sb("mhalf", [P, TT], F32)
        gw = sb("gw", [P, E], F32)
        logit = sb("logit", [P, TT, E], F32)
        lmax = sb("lmax", [P, TT], F32)
        lexp = sb("lexp", [P, TT, E], F32)
        prob = sb("prob", [P, TT], F32)
        cand = sb("cand", [P, TT, E], F32)
        iota_e = sb("iota_e", [P, TT, E], F32)
        first = sb("first", [P, TT], F32)
        hot_padded = sb("hot_padded", [P, 2 * TT, E], BF16)
        hot = hot_padded[:, TT:2 * TT, :]
        tri = sb("tri", [P, P], BF16)
        ones_bf = sb("ones_bf", [P, P], BF16)
        pose = sb("pose", [P, TT, E], F32)
        pos = sb("pos", [P, TT], F32)
        slotf = sb("slotf", [P, TT], F32)
        slot = sb("slot", [P, TT], U32)
        w1s = sb("w1s", [P, E, F], F32)
        with ExitStack() as early:
            xT_hi = early.enter_context(nc.sbuf_tensor("xT_hi", [P, TT * P], F32R))
            xT_lo = early.enter_context(nc.sbuf_tensor("xT_lo", [P, TT * P], F32R))
        w2s = sb("w2s", [P, E, FT, D], F32)
        tok = OT
        p32 = P32[:].rearrange("p h n -> p (h n)")
        tT = p32
        fetched = parts32[:, 0:TT * D].rearrange("p (t d) -> p t d", d=D)
        xe = parts32[:, TT * D:TT * D + SLOTS].rearrange("p (t d) -> p t d", d=D)
        xeT = O[:].rearrange("p q n -> p (q n)")[:, 0:SLOTS]
        hT = VL[:].rearrange("p k h d -> p (k h d)").bitcast(F32)[:, 0:2 * FT * CAP]\
            .rearrange("p (b f c) -> p b f c", b=2, f=FT)
        yT = VH[:].rearrange("p k h d -> p (k h d)").bitcast(F32)[:, 0:SLOTS]
        yrows = p32[:, 0:SLOTS].rearrange("p (t d) -> p t d", d=D)
        zeros = O[:].rearrange("p q n -> p (q n)")

        psS = [pb(f"psS{i}", [P, 512]) for i in range(2)]
        psM = pb("psM", [P, QT, 512])
        psKQ = pb("psKQ", [P, 1024])
        psO = pb("psO", [P, 512])
        psX = pb("psX", [P, 512])

        x_in = sem("x_in")
        small_in = sem("small_in")
        w_in = sem("w_in")
        wo_in = sem("wo_in")
        ctx_in = sem("ctx_in")
        exp_w_in = sem("exp_w_in")
        w2_in = sem("w2_in")
        ident_zero = sem("ident_zero")
        ident_ready = sem("ident_ready")
        pool_consts = sem("pool_consts")
        stack_consts = sem("stack_consts")
        stats_done = sem("stats_done")
        mv_done = sem("mv_done")
        vv_done = sem("vv_done")
        rstd_done = sem("rstd_done")
        xn_done = sem("xn_done")
        w_hi_done = sem("w_hi_done")
        w_lo_done = sem("w_lo_done")
        xt_psum = sem("xt_psum")
        xt_f32 = sem("xt_f32")
        xt_hi_done = sem("xt_hi_done")
        xt_lo_done = sem("xt_lo_done")
        ctxt_psum = sem("ctxt_psum")
        ctxt_hi_done = sem("ctxt_hi_done")
        ctxt_lo_done = sem("ctxt_lo_done")
        kq_psum = sem("kq_psum")
        kq_hi_done = sem("kq_hi_done")
        kq_lo_done = sem("kq_lo_done")
        stack_in = [sem(f"stack_in{i}") for i in range(BUFS)]
        smax_psum = sem("smax_psum")
        max_done = sem("max_done")
        mt_psum = sem("mt_psum")
        mxs_hi_done = sem("mxs_hi_done")
        mxs_lo_done = sem("mxs_lo_done")
        mrow_done = sem("mrow_done")
        mrow_in = [sem(f"mrow_in{i}") for i in range(2)]
        score_psum = sem("score_psum")
        exp_done = sem("exp_done")
        phi0_done = sem("phi0_done")
        phi1_done = sem("phi1_done")
        plo_done = sem("plo_done")
        v_psum = sem("v_psum")
        v_hi_done = sem("v_hi_done")
        v_lo_done = sem("v_lo_done")
        pv_done = sem("pv_done")
        rden_done = sem("rden_done")
        norm_done = sem("norm_done")
        ot_psum = sem("ot_psum")
        ot_done = sem("ot_done")
        proj_psum = sem("proj_psum")
        x1_done = sem("x1_done")
        tgate_done = sem("tgate_done")
        gscale_done = sem("gscale_done")
        zeros_done = sem("zeros_done")
        zeros_out = sem("zeros_out")
        tok_done = sem("tok_done")
        tokt_psum = sem("tokt_psum")
        tokt_done = sem("tokt_done")
        logit_psum = sem("logit_psum")
        route = sem("route")
        lexp_done = sem("lexp_done")
        pos_psum = sem("pos_psum")
        slot_done = sem("slot_done")
        scattered = sem("scattered")
        xe_in = sem("xe_in")
        xet_psum = sem("xet_psum")
        xet_done = sem("xet_done")
        h_psum = sem("h_psum")
        h_done = sem("h_done")
        y_psum = sem("y_psum")
        y_done = sem("y_done")
        yrow_psum = sem("yrow_psum")
        yrow_done = sem("yrow_done")
        ye_out = sem("ye_out")
        fetch_zero = sem("fetch_zero")
        gathered = sem("gathered")
        final_done = sem("final_done")
        out_done = sem("out_done")

        x_t = x.rearrange("b (t p) d -> p (b t) d", p=P)
        out_t = out.rearrange("b (t p) d -> p (b t) d", p=P)
        ctx_t = ctx_1024.rearrange("b (t p) d -> b p t d", p=P)

        def slots(b):
            for hp in range(PAIRS):
                yield b * PAIRS + hp, hp

        def back(b, hp, k):
            return (b, hp - k) if hp >= k else (b - 1, hp - k + PAIRS)

        def is_last(b):
            return isinstance(b, int) and b == B - 1

        def is_first(b):
            return isinstance(b, int) and b == 0

        def each_batch(eng, body):
            body(0)
            with eng.Fori(1, B - 1) as b:
                body(b)
            body(B - 1)

        def stack_value(b, hp):
            return b * (64 * PAIRS // BUFS) + 64 * (hp // BUFS + 1)

        def mrow_value(b, hp):
            return b * (32 * PAIRS // 2) + 32 * (hp // 2 + 1)

        def v_group(b, hp):
            if hp < KT:
                return (b, 1, hp)
            return None if is_last(b) else (b + 1, 0, hp - KT)

        OT_STEPS = {4: (0, 0), 6: (0, 1), 0: (1, 2), 1: (1, 3)}

        def ot_group(b, hp):
            if hp not in OT_STEPS or (is_first(b) and OT_STEPS[hp][0]):
                return None
            return (b - OT_STEPS[hp][0], OT_STEPS[hp][1])

        PROJECT_STEP = 2
        CTX_STEP = KT - 1

        def next_pair(b, hp, k):
            return (b, hp + k) if hp + k < PAIRS else (b + 1, hp + k - PAIRS)

        block = ctx.enter_context(nc.Block())

        @block.sync
        def _(sp):
            sp.dma_start(X1[:], x_t).then_inc(x_in, 16)
            sp.dma_start(ctx_raw[:], ctx_t[0]).then_inc(ctx_in, 16)
            sp.dma_start(wraw[:, 0:INNER], w_q).then_inc(w_in, 16)
            sp.dma_start(wraw[:, INNER:3 * INNER], w_kv).then_inc(w_in, 16)
            sp.dma_start(gamma[:], ln_gamma.rearrange("(p o) -> p o", o=1)).then_inc(small_in, 16)
            sp.dma_start(beta[:], ln_beta.rearrange("(p o) -> p o", o=1)).then_inc(small_in, 16)
            for i, g in enumerate((g_xattn, gate, g_ffn)):
                sp.dma_start(gates[:, i:i + 1], g.rearrange("(o n) -> o n", o=1).to_broadcast([P, 1])).then_inc(small_in, 16)
            sp.dma_start(bo[:], b_out.rearrange("(o n) -> o n", o=1)).then_inc(wo_in, 16)
            sp.dma_start(wo[:], w_out.rearrange("(c p) n -> p c n", p=P)).then_inc(wo_in, 16)
            sp.dma_start(gw[:], gate_w).then_inc(exp_w_in, 16)
            sp.dma_start(w1s[:], w1.rearrange("e d f -> d e f")).then_inc(exp_w_in, 16)
            sp.wait_ge(zeros_done, 1)
            sp.dma_start(xe_dram.rearrange("(p t) d -> p (t d)", p=P), zeros[:, 0:SLOTS]).then_inc(zeros_out, 16)

            def stacks(b, hp):
                j = b * PAIRS + hp
                buf, par = hp % BUFS, hp % 2
                sp.wait_ge(kq_lo_done, 2 * j + 2)
                sp.wait_ge(kq_hi_done, 2 * j + 2)
                if not (is_first(b) and hp < BUFS):
                    sp.wait_ge(score_psum, 4 * j - 4 * (BUFS - 1))
                for h in range(2):
                    parts = HL[64 * h:64 * h + 64, par, :].bitcast(F32)
                    both = bass.AP(parts.tensor, parts.offset, [parts.ap[0], [SQ, 2], [1, KQ]])
                    sp.dma_start(ST[0:64, buf, h, :].bitcast(F32).rearrange("p (g n) -> p g n", g=2), both)\
                      .then_inc(stack_in[buf], 16)
                    sp.dma_start(ST[64:128, buf, h, AK:STW].bitcast(F32), parts[:, H_KLO:H_KLO + KQ])\
                      .then_inc(stack_in[buf], 16)

            def max_rows(b, hp):
                j = b * PAIRS + hp
                buf, par = hp % BUFS, hp % 2
                sp.wait_ge(mrow_done, j + 1)
                for h in range(2):
                    sp.dma_start(ST[64:66, buf, h, BQ:BK].bitcast(F32), MROW[2 * h:2 * h + 2, par, :].bitcast(F32))\
                      .then_inc(mrow_in[par], 16)

            sp.wait_ge(stack_consts, 4)
            for hp in range(AHEAD):
                stacks(0, hp)
            max_rows(0, 0)

            def batch(b):
                for j, hp in slots(b):
                    if hp == 0 and not is_last(b):
                        sp.wait_ge(ctxt_psum, b + 1)
                        sp.dma_start(ctx_raw[:], ctx_t[b + 1]).then_inc(ctx_in, 16)
                    if not (is_last(b) and hp + 1 >= PAIRS):
                        max_rows(*next_pair(b, hp, 1))
                    if not (is_last(b) and hp + AHEAD >= PAIRS):
                        stacks(*next_pair(b, hp, AHEAD))

            each_batch(sp, batch)

            sp.wait_ge(kq_psum, B * PAIRS)
            sp.dma_start(w2s[:], w2.rearrange("e (c p) d -> p e c d", p=P)).then_inc(w2_in, 16)
            sp.wait_ge(scattered, 16 * TT)
            sp.dma_start(xe, xe_dram.rearrange("(t p) d -> p t d", p=P)).then_inc(xe_in, 16)
            sp.wait_ge(yrow_done, 3)
            sp.dma_start(ye_dram.rearrange("(t p) d -> p t d", p=P), yrows).then_inc(ye_out, 16)
            sp.wait_ge(final_done, TT)
            sp.dma_start(out_t, X1[:]).then_inc(out_done, 16)
            sp.wait_ge(out_done, 16)

        @block.gpsimd
        def _(pool):
            pool.memset(ident[:], 0.0).then_inc(ident_zero, 1)
            pool.wait_ge(ident_zero, 1)
            pool.affine_select(out=ident[:], in_=ident[:], compare_op=ALU.not_equal, fill=1.0, base=0,
                               pattern=[[-1, P]], channel_multiplier=1).then_inc(ident_ready, 1)
            pool.memset(mhalf[:], -0.5).then_inc(pool_consts, 1)
            pool.memset(ones1[:], 1.0).then_inc(pool_consts, 1)
            pool.wait_ge(vv_done, 1)
            pool.wait_ge(pool_consts, 1)
            pool.tensor_tensor(rstd[:], vv[:], mhalf[:], ALU.pow).then_inc(rstd_done, 1)
            pool.memset(zeros[:, 0:SLOTS], 0.0).then_inc(zeros_done, 1)
            pool.memset(ones_bf[:], 1.0).then_inc(ident_zero, 1)
            pool.wait_ge(ident_zero, 2)
            pool.affine_select(out=tri[:], in_=ones_bf[:], compare_op=ALU.is_ge, fill=0.0, base=0,
                               pattern=[[1, P]], channel_multiplier=-1).then_inc(pool_consts, 1)
            pool.iota(iota_e[:], pattern=[[0, TT], [1, E]], base=-E, channel_multiplier=0,
                      allow_small_or_imprecise_dtypes=True).then_inc(ident_zero, 1)

            def batch(b):
                for j, hp in slots(b):
                    for h in range(2):
                        par = hp % 2
                        pool.wait_ge(exp_done, 4 * j + 2 * h + 2)
                        pool.wait_ge(phi0_done if h == 0 else phi1_done, j + 1)
                        if not (is_first(b) and hp < 2):
                            pool.wait_ge(pv_done, 2 * j - 4 + h + 1)
                        pool.tensor_tensor(PLO[:, par, h, :], P32[:, h, :], PHI[:, par, h, :],
                                           ALU.subtract).then_inc(plo_done, 1)

            each_batch(pool, batch)

            pool.wait_ge(plo_done, 2 * B * PAIRS)
            pool.wait_ge(pv_done, 2 * B * PAIRS)
            pool.memset(fetched, 0.0).then_inc(fetch_zero, 1)
            pool.wait_ge(vv_done, 2)
            pool.tensor_tensor(rstd[:], vv[:], mhalf[:], ALU.pow).then_inc(rstd_done, 1)
            pool.wait_ge(slot_done, 1)
            pool.wait_ge(zeros_out, 16)
            for t in range(TT):
                pool.indirect_dma_start(out=xe_dram, out_offset=bass.IndirectOffsetOnAxis(slot[:, t:t + 1], 0),
                                        in_=tok[:, t, :], in_offset=None, bounds_check=SLOTS - 1,
                                        oob_is_err=False).then_inc(scattered, 16)
            pool.wait_ge(ye_out, 16)
            pool.wait_ge(fetch_zero, 1)
            for t in range(TT):
                pool.indirect_dma_start(out=fetched[:, t, :], out_offset=None, in_=ye_dram,
                                        in_offset=bass.IndirectOffsetOnAxis(slot[:, t:t + 1], 0),
                                        bounds_check=SLOTS - 1, oob_is_err=False).then_inc(gathered, 16)

        @block.scalar
        def _(act):
            act.wait_ge(small_in, 80)
            act.activation(tgates[:], gates[:], ACT.Tanh).then_inc(tgate_done, 1)
            act.wait_ge(w_in, 32)
            for c in range(3):
                cs = slice(c * INNER, (c + 1) * INNER)
                act.activation(w_hi[:, cs], wraw[:, cs], ACT.Copy).then_inc(w_hi_done, 1)
            for i in range(TT // 4):
                cs = slice(512 * i, 512 * i + 512)
                act.wait_ge(xt_psum, i + 1)
                if i:
                    act.wait_ge(xt_lo_done, i)
                act.activation(P32[:, 0, 0:512], psX[:], ACT.Identity, bias=beta[:, 0:1],
                               scale=gamma[:, 0:1]).then_inc(xt_f32, 1)
                act.wait_ge(xt_f32, i + 1)
                act.activation(xT_hi[:, cs], P32[:, 0, 0:512], ACT.Copy).then_inc(xt_hi_done, 1)

            def ctxt_hi(b):
                act.wait_ge(ctxt_psum, b + 1)
                act.activation(cT_hi[:], psX[:], ACT.Copy).then_inc(ctxt_hi_done, 1)

            def kq_hi(b, hp):
                j = b * PAIRS + hp
                act.wait_ge(kq_psum, j + 1)
                if not (is_first(b) and hp < 2):
                    pb_, php = (b, hp - 2) if hp >= 2 else (b - 1, hp - 2 + PAIRS)
                    act.wait_ge(stack_in[php % BUFS], stack_value(pb_, php))
                act.activation(HL[:, hp % 2, H_KHI:H_KHI + KQ], psKQ[:, 0:KQ], ACT.Copy).then_inc(kq_hi_done, 1)
                act.activation(HL[:, hp % 2, H_QHI2:H_QHI2 + SQ], psKQ[:, SK:KQ], ACT.Copy).then_inc(kq_hi_done, 1)

            def max_row(b, hp):
                j = b * PAIRS + hp
                act.wait_ge(mt_psum, j + 1)
                if not (is_first(b) and hp < 2):
                    act.wait_ge(mrow_in[hp % 2], mrow_value(*back(b, hp, 2)))
                act.activation(MROW[:, hp % 2, :], psKQ[0:4, KQ:KQ + SQ], ACT.Copy).then_inc(mrow_done, 1)

            def v_hi(b, half, kt):
                n = b * 2 * KT + half * KT + kt
                act.wait_ge(v_psum, n + 1)
                act.activation(VH[:, kt, 8 * half:8 * half + 8, 0:DH],
                               psX[:].rearrange("p (h d) -> p h d", d=DH), ACT.Copy).then_inc(v_hi_done, 1)

            def ot_copy(b, i):
                act.wait_ge(ot_psum, b * 4 + i + 1)
                if not (is_first(b)):
                    act.wait_ge(proj_psum, b)
                act.activation(OT[:, 4 * i:4 * i + 4, :], psX[:].rearrange("p (t c) -> p t c", c=P),
                               ACT.Copy).then_inc(ot_done, 1)

            def exps(j, c, first_pairs):
                h = c // 2
                act.wait_ge(score_psum, 4 * j + c + 1)
                if not (first_pairs):
                    act.wait_ge(plo_done, 2 * j - 2 + h + 1)
                act.activation(P32[:, h, 512 * (c % 2):512 * (c % 2) + 512], psS[c % 2][:], ACT.Exp,
                               scale=SCALE).then_inc(exp_done, 1)

            ctxt_hi(0)
            for hp in range(AHEAD):
                kq_hi(0, hp)
            for kt in range(KT):
                v_hi(0, 0, kt)
            max_row(0, 0)
            act.wait_ge(xt_lo_done, TT // 4)

            def batch(b):
                for j, hp in slots(b):
                    start = is_first(b) and hp == 0
                    exps(j, 0, start)
                    if not (is_last(b) and hp + 1 >= PAIRS):
                        max_row(*next_pair(b, hp, 1))
                    exps(j, 1, start)
                    if not (is_last(b) and hp + AHEAD >= PAIRS):
                        kq_hi(*next_pair(b, hp, AHEAD))
                    if ot_group(b, hp):
                        ot_copy(*ot_group(b, hp))
                    if hp == CTX_STEP:
                        v_hi(*v_group(b, hp))
                    exps(j, 2, start)
                    exps(j, 3, start)
                    act.wait_ge(exp_done, 4 * j + 4)
                    if not (is_first(b) and hp < 2):
                        act.wait_ge(pv_done, 2 * j - 2)
                    act.activation(PHI[:, hp % 2, 1, :], P32[:, 1, :], ACT.Copy).then_inc(phi1_done, 1)
                    if v_group(b, hp) and hp != CTX_STEP:
                        v_hi(*v_group(b, hp))
                    if hp == CTX_STEP and not is_last(b):
                        ctxt_hi(b + 1)

            each_batch(act, batch)
            ot_copy(B - 1, 2)
            ot_copy(B - 1, 3)

            for i in range(TT // 4):
                act.wait_ge(tokt_psum, i + 1)
                act.activation(tT[:, 512 * i:512 * i + 512], psS[i % 2][:], ACT.Copy).then_inc(tokt_done, 1)
            act.wait_ge(route, 2)
            act.activation(lexp[:], cand[:], ACT.Exp).then_inc(lexp_done, 1)
            for i in range(3):
                n = min(4, ST_TILES - 4 * i)
                act.wait_ge(xet_psum, i + 1)
                act.activation(xeT[:, 512 * i:512 * i + n * P], psS[i % 2][:, 0:n * P], ACT.Copy).then_inc(xet_done, 1)
            for e in range(E):
                for i in range(2):
                    act.wait_ge(h_psum, 2 * e + i + 1)
                    if e >= 2:
                        act.wait_ge(y_psum, e - 1)
                    act.activation(hT[:, e % 2, 2 * i:2 * i + 2, :],
                                   psM[:, i, 0:2 * CAP].rearrange("p (f c) -> p f c", f=2), ACT.Relu).then_inc(h_done, 1)

        @block.vector
        def _(dve):
            dve.memset(ST[:].bitcast(F32)[64:128, :, :, BK:AK], 1.0).then_inc(stack_consts, 1)
            dve.memset(ST[:].bitcast(F32)[64:128, :, :, BQ:BK], LIFT).then_inc(stack_consts, 1)
            dve.memset(VH[:], 1.0).then_inc(stack_consts, 1)
            dve.memset(hot_padded[:, 0:TT, :], 0.0).then_inc(stack_consts, 1)

            def normalise(n, dst):
                for t in range(TT):
                    dve.bn_stats(stats[:, t, :], X1[:, t, :]).then_inc(stats_done, 1)
                for t in range(TT):
                    dve.wait_ge(stats_done, TT * n + t + 1)
                    dve.bn_aggr(mv[:, t, :], stats[:, t, :]).then_inc(mv_done, 1)
                dve.wait_ge(mv_done, TT * n + TT)

            dve.wait_ge(x_in, 16)
            normalise(0, None)
            dve.tensor_scalar(vv[:], mv[:, :, 1], 1.0 + EPS, EPS * EPS, ALU.mult, ALU.add).then_inc(vv_done, 1)
            dve.wait_ge(rstd_done, 1)
            for t in range(TT):
                dve.tensor_scalar(OT[:, t, :], X1[:, t, :], mv[:, t, 0:1], rstd[:, t:t + 1], ALU.subtract,
                                  ALU.mult).then_inc(xn_done, 1)
            for c in range(3):
                cs = slice(c * INNER, (c + 1) * INNER)
                dve.wait_ge(w_hi_done, c + 1)
                dve.tensor_tensor(w_lo[:, cs], wraw[:, cs], w_hi[:, cs].bitcast(F32), ALU.subtract).then_inc(w_lo_done, 1)
            for i in range(TT // 4):
                cs = slice(512 * i, 512 * i + 512)
                dve.wait_ge(xt_hi_done, i + 1)
                dve.tensor_tensor(xT_lo[:, cs], P32[:, 0, 0:512], xT_hi[:, cs].bitcast(F32), ALU.subtract)\
                   .then_inc(xt_lo_done, 1)
            dve.wait_ge(tgate_done, 1)
            dve.tensor_tensor(gscale[:], tgates[:, 0:1], tgates[:, 1:2], ALU.mult).then_inc(gscale_done, 1)

            def ctxt_lo(b):
                dve.wait_ge(ctxt_hi_done, b + 1)
                dve.tensor_tensor(cT_lo[:], psX[:], cT_hi[:].bitcast(F32), ALU.subtract).then_inc(ctxt_lo_done, 1)

            def kq_lo(b, hp):
                j = b * PAIRS + hp
                dve.wait_ge(kq_hi_done, 2 * j + 2)
                hl = HL[:, hp % 2, :]
                dve.tensor_tensor(hl[:, H_KLO:H_KLO + SK], psKQ[:, 0:SK],
                                  hl[:, H_KHI:H_KHI + SK].bitcast(F32), ALU.subtract).then_inc(kq_lo_done, 1)
                dve.tensor_tensor(hl[:, H_QLO:H_QLO + SQ], psKQ[:, SK:KQ],
                                  hl[:, H_QHI:H_QHI + SQ].bitcast(F32), ALU.subtract).then_inc(kq_lo_done, 1)

            def v_lo(b, half, kt):
                n = b * 2 * KT + half * KT + kt
                dve.wait_ge(v_hi_done, n + 1)
                dve.tensor_tensor(VL[:, kt, 8 * half:8 * half + 8, :], psX[:].rearrange("p (h d) -> p h d", d=DH),
                                  VH[:, kt, 8 * half:8 * half + 8, 0:DH], ALU.subtract).then_inc(v_lo_done, 1)

            def row_max(b, hp, h):
                j = b * PAIRS + hp
                dve.wait_ge(smax_psum, 2 * j + h + 1)
                if not (is_first(b) and hp < 2):
                    dve.wait_ge(mt_psum, j - 1)
                dve.tensor_reduce(MX[:, hp % 2, h, :], psM[:], AX.X, ALU.max).then_inc(max_done, 1)

            def split_max(b, hp):
                j = b * PAIRS + hp
                maxima = MX[:, hp % 2].rearrange("p h q -> p q h")
                hi, lo = MXS[:, hp % 2, :, :, 0], MXS[:, hp % 2, :, :, 1]
                dve.wait_ge(max_done, 2 * j + 2)
                dve.tensor_scalar(hi, maxima, -1.0, None, ALU.mult).then_inc(mxs_hi_done, 1)
                dve.wait_ge(mxs_hi_done, j + 1)
                dve.scalar_tensor_tensor(out=lo, in0=maxima, scalar=-1.0, in1=hi.bitcast(F32), op0=ALU.mult,
                                         op1=ALU.subtract).then_inc(mxs_lo_done, 1)

            def normalise_heads(b, hp, start_of_all):
                j = b * PAIRS + hp
                sums = psO[:, 0:2 * QT * (DH + 1)].rearrange("p (g d) -> p g d", d=DH + 1)
                dve.wait_ge(pv_done, 2 * j + 2)
                dve.reciprocal(rden[:, hp % 2, :], sums[:, :, DH]).then_inc(rden_done, 1)
                dve.wait_ge(rden_done, j + 1)
                if hp % 2 == 0 and not is_first(b):
                    dve.wait_ge(ot_psum, b * 4 - 4 + hp // 2 + 1)
                if start_of_all:
                    dve.wait_ge(zeros_out, 16)
                o = O[:, :, P * hp:P * hp + P].rearrange("p q (h d) -> p h q d", h=2)
                dve.tensor_tensor(o, sums[:, :, 0:DH].rearrange("p (h q) d -> p h q d", h=2),
                                  rden[:, hp % 2, :].rearrange("p (h q) -> p h q", h=2).unsqueeze(3)
                                  .to_broadcast([P, 2, QT, DH]), ALU.mult).then_inc(norm_done, 1)

            def add_attention(b):
                dve.wait_ge(proj_psum, b + 1)
                xs = X1[:, bass.ds(b * QT, QT), :]
                dve.scalar_tensor_tensor(out=xs, in0=psX[:, 0:QT * D].rearrange("p (q d) -> p q d", q=QT),
                                         scalar=gscale[:, 0:1], in1=xs, op0=ALU.mult, op1=ALU.add).then_inc(x1_done, 1)

            ctxt_lo(0)
            for hp in range(AHEAD):
                kq_lo(0, hp)
            for kt in range(KT):
                v_lo(0, 0, kt)
            for hp in range(2):
                row_max(0, hp, 0)
                row_max(0, hp, 1)
                split_max(0, hp)
            dve.wait_ge(gscale_done, 1)

            def batch(b):
                for j, hp in slots(b):
                    more2 = not (is_last(b) and hp + 2 >= PAIRS)
                    dve.wait_ge(exp_done, 4 * j + 2)
                    if not (is_first(b) and hp < 2):
                        dve.wait_ge(pv_done, 2 * j - 3)
                    dve.tensor_copy(PHI[:, hp % 2, 0, :], P32[:, 0, :]).then_inc(phi0_done, 1)
                    if more2:
                        row_max(*next_pair(b, hp, 2), 0)
                    if not (is_last(b) and hp + AHEAD >= PAIRS):
                        kq_lo(*next_pair(b, hp, AHEAD))
                    if hp == PROJECT_STEP and not is_first(b):
                        add_attention(b - 1)
                    if hp == CTX_STEP:
                        v_lo(*v_group(b, hp))
                    if not (is_first(b) and hp == 0):
                        normalise_heads(*back(b, hp, 1), is_first(b) and hp == 1)
                    if more2:
                        row_max(*next_pair(b, hp, 2), 1)
                        split_max(*next_pair(b, hp, 2))
                    if v_group(b, hp) and hp != CTX_STEP:
                        v_lo(*v_group(b, hp))
                    if hp == CTX_STEP and not is_last(b):
                        ctxt_lo(b + 1)

            each_batch(dve, batch)
            normalise_heads(B - 1, PAIRS - 1, False)
            add_attention(B - 1)

            dve.wait_ge(x1_done, B)
            normalise(1, None)
            dve.tensor_scalar(vv[:], mv[:, :, 1], EPS, None, ALU.add).then_inc(vv_done, 1)
            dve.wait_ge(rstd_done, 2)
            for t in range(TT):
                dve.tensor_scalar(tok[:, t, :], X1[:, t, :], mv[:, t, 0:1], rstd[:, t:t + 1], ALU.subtract,
                                  ALU.mult).then_inc(tok_done, 1)

            def wide(a):
                return a.unsqueeze(2).to_broadcast([P, TT, E])

            step = [0]

            def then(ins):
                step[0] += 1
                ins.then_inc(route, 1)
                dve.wait_ge(route, step[0])

            lg = psX[:, 0:TT * E].rearrange("p (t e) -> p t e", e=E)
            dve.wait_ge(logit_psum, 1)
            then(dve.tensor_reduce(lmax[:], lg, AX.X, ALU.max))
            then(dve.tensor_tensor(cand[:], lg, wide(lmax[:]), ALU.subtract))
            dve.wait_ge(ident_zero, 3)
            then(dve.scalar_tensor_tensor(out=logit[:], in0=cand[:], scalar=0.0, in1=iota_e[:],
                                          op0=ALU.is_equal, op1=ALU.mult))
            then(dve.tensor_reduce(first[:], logit[:], AX.X, ALU.min))
            then(dve.tensor_tensor(hot, iota_e[:], wide(first[:]), ALU.is_equal))
            dve.wait_ge(lexp_done, 1)
            then(dve.tensor_reduce(lmax[:], lexp[:], AX.X, ALU.add))
            then(dve.reciprocal(prob[:], lmax[:]))
            then(dve.tensor_scalar(prob[:], prob[:], tgates[:, 2:3], None, ALU.mult))
            dve.wait_ge(pos_psum, 1)
            then(dve.tensor_tensor(pose[:], psO[:, 0:TT * E].rearrange("p (t e) -> p t e", e=E), hot, ALU.mult))
            then(dve.tensor_reduce(pos[:], pose[:], AX.X, ALU.add))
            then(dve.tensor_scalar(slotf[:], first[:], float(CAP), float(E * CAP - 1), ALU.mult, ALU.add))
            then(dve.tensor_tensor(slotf[:], slotf[:], pos[:], ALU.add))
            then(dve.tensor_scalar(pos[:], pos[:], float(CAP), DROPPED, ALU.is_gt, ALU.mult))
            dve.tensor_tensor(slot[:], slotf[:], pos[:], ALU.add).then_inc(slot_done, 1)

            for e in range(E):
                dve.wait_ge(y_psum, e + 1)
                dve.tensor_copy(yT[:, e * CAP:(e + 1) * CAP], [psO, psX][e % 2][:, 0:CAP]).then_inc(y_done, 1)
            for i in range(3):
                n = min(4, ST_TILES - 4 * i)
                dve.wait_ge(yrow_psum, i + 1)
                dve.tensor_copy(yrows[:, 4 * i:4 * i + n, :],
                                psS[i % 2][:, 0:n * P].rearrange("p (t d) -> p t d", d=D)).then_inc(yrow_done, 1)
            dve.wait_ge(gathered, 16 * TT)
            for t in range(TT):
                dve.scalar_tensor_tensor(out=X1[:, t, :], in0=fetched[:, t, :], scalar=prob[:, t:t + 1],
                                         in1=X1[:, t, :], op0=ALU.mult, op1=ALU.add).then_inc(final_done, 1)

        @block.tensor
        def _(pe):
            def matmul3(dst, hi_l, lo_l, hi_r, lo_r):
                pe.matmul(dst, hi_l, hi_r, start=True, stop=False)
                pe.matmul(dst, hi_l, lo_r, start=False, stop=False)
                return pe.matmul(dst, lo_l, hi_r, start=False, stop=True)

            x_free = [None]

            def wait_x(free_when):
                if x_free[0]:
                    pe.wait_ge(*x_free[0])
                x_free[0] = free_when

            def ctx_transposes(b):
                pe.wait_ge(ctx_in, 16 * b + 16)
                wait_x((ctxt_lo_done, b + 1))
                for kt in range(KT):
                    last = pe.transpose(psX[:, P * kt:P * kt + P], ctx_raw[:, kt, :], ident[:])
                last.then_inc(ctxt_psum, 1)

            def k_project(b, hp):
                j = b * PAIRS + hp
                if not (is_first(b) and hp == 0):
                    pe.wait_ge(kq_lo_done, 2 * j)
                if hp == 0:
                    pe.wait_ge(ctxt_lo_done, b + 1)
                k_cols = slice(INNER + P * hp, INNER + P * hp + P)
                matmul3(psKQ[:, 0:SK], w_hi[:, k_cols], w_lo[:, k_cols], cT_hi[:], cT_lo[:])

            def q_project(b, hp):
                if not (is_first(b) and hp < AHEAD):
                    pe.wait_ge(mrow_done, b * PAIRS + hp - AHEAD + 2)
                q_cols = slice(P * hp, P * hp + P)
                xs = bass.ds(b * SQ, SQ)
                matmul3(psKQ[:, SK:KQ], w_hi[:, q_cols], w_lo[:, q_cols], xT_hi[:, xs], xT_lo[:, xs])\
                    .then_inc(kq_psum, 1)

            def v_project(b, half, kt):
                wait_x((v_lo_done, b * 2 * KT + half * KT + kt + 1))
                pe.wait_ge(ctxt_lo_done, b + 1)
                cs = slice(P * kt, P * kt + P)
                ws = slice(2 * INNER + 512 * half, 2 * INNER + 512 * half + 512)
                matmul3(psX[:], cT_hi[:, cs], cT_lo[:, cs], w_hi[:, ws], w_lo[:, ws]).then_inc(v_psum, 1)

            def max_scores(b, hp, h):
                j = b * PAIRS + hp
                buf = hp % BUFS
                if h == 0:
                    pe.wait_ge(stack_in[buf], stack_value(b, hp))
                if not (is_first(b) and hp == 0 and h == 0):
                    pe.wait_ge(max_done, 2 * j + h)
                for qt in range(QT):
                    last = pe.matmul(psM[:, qt, :], ST[:, buf, h, AQ + P * qt:AQ + P * qt + P],
                                     ST[:, buf, h, AK:AQ], start=True, stop=True)
                last.then_inc(smax_psum, 1)

            def max_transpose(b, hp, kq_before):
                j = b * PAIRS + hp
                pe.wait_ge(mxs_lo_done, j + 1)
                pe.wait_ge(kq_lo_done, 2 * kq_before)
                for qt in range(QT):
                    maxima = MXS[:, hp % 2, qt].bitcast(F32).rearrange("p h r -> p (h r)")
                    last = pe.transpose(psKQ[0:4, KQ + P * qt:KQ + P * qt + P], maxima, ident[:])
                last.then_inc(mt_psum, 1)

            def scores(b, hp, c):
                j = b * PAIRS + hp
                buf, h = hp % BUFS, c // 2
                if c == 0:
                    pe.wait_ge(mrow_in[hp % 2], mrow_value(b, hp))
                if not (is_first(b) and hp == 0 and c < 2):
                    pe.wait_ge(exp_done, 4 * j + c - 1)
                for i in range(2):
                    kt = 2 * (c % 2) + i
                    dst = psS[c % 2][:, SQ * i:SQ * i + SQ]
                    pe.matmul(dst, ST[:, buf, h, AK + P * kt:AK + P * kt + P], ST[:, buf, h, AQ:STW], start=True, stop=False)
                    last = pe.matmul(dst, ST[:, buf, h, BK + P * kt:BK + P * kt + P], ST[:, buf, h, BQ:BK],
                                     start=False, stop=True)
                last.then_inc(score_psum, 1)

            def values(b, hp, h):
                j = b * PAIRS + hp
                par, head = hp % 2, 2 * hp + h
                pe.wait_ge(plo_done, 2 * j + h + 1)
                if h == 0:
                    if not (is_first(b) and hp == 0):
                        pe.wait_ge(norm_done, j)
                    if hp % 4 == 0:
                        pe.wait_ge(v_lo_done, b * 2 * KT + KT * (hp // 4 + 1))
                for qt in range(QT):
                    g = (h * QT + qt) * (DH + 1)
                    for kt in range(KT):
                        cs = slice(SQ * kt + P * qt, SQ * kt + P * qt + P)
                        phi, plo = PHI[:, par, h, cs], PLO[:, par, h, cs]
                        first_, last_ = kt == 0, kt == KT - 1
                        pe.matmul(psO[:, g:g + DH + 1], phi, VH[:, kt, head, 0:DH + 1], start=first_, stop=False)
                        pe.matmul(psO[:, g:g + DH], phi, VL[:, kt, head, :], start=False, stop=False)
                        last = pe.matmul(psO[:, g:g + DH + 1], plo, VH[:, kt, head, 0:DH + 1], start=False,
                                         stop=last_)
                last.then_inc(pv_done, 1)

            def o_transposes(b, i):
                wait_x((ot_done, b * 4 + i + 1))
                pe.wait_ge(norm_done, b * PAIRS + 2 * i + 2)
                for n in range(4):
                    pair, qt = divmod(4 * i + n, QT)
                    last = pe.transpose(psX[:, P * n:P * n + P], O[:, qt, P * pair:P * pair + P], ident[:])
                last.then_inc(ot_psum, 1)

            def project(b):
                wait_x((x1_done, b + 1))
                pe.wait_ge(ot_done, b * 4 + 4)
                for qt in range(QT):
                    dst = psX[:, D * qt:D * qt + D]
                    pe.matmul(dst, ones1[:], bo[:], start=True, stop=False)
                    for pair in range(PAIRS):
                        last = pe.matmul(dst, OT[:, pair * QT + qt, :], wo[:, pair, :], start=False,
                                         stop=(pair == PAIRS - 1))
                last.then_inc(proj_psum, 1)

            pe.wait_ge(ident_ready, 1)
            for i in range(TT // 4):
                wait_x((xt_f32, i + 1))
                for n in range(4):
                    pe.wait_ge(xn_done, 4 * i + n + 1)
                    last = pe.transpose(psX[:, P * n:P * n + P], OT[:, 4 * i + n, :], ident[:])
                last.then_inc(xt_psum, 1)
            ctx_transposes(0)
            pe.wait_ge(w_lo_done, 3)
            pe.wait_ge(xt_lo_done, TT // 4)
            for hp in range(AHEAD):
                k_project(0, hp)
                q_project(0, hp)
            pe.wait_ge(stack_consts, 4)
            for kt in range(KT):
                v_project(0, 0, kt)
            for hp in range(2):
                for h in range(2):
                    max_scores(0, hp, h)
            max_transpose(0, 0, AHEAD)
            pe.wait_ge(wo_in, 32)

            def batch(b):
                if not is_first(b):
                    x_free[0] = (v_lo_done, b * 2 * KT + KT)
                for j, hp in slots(b):
                    more1 = not (is_last(b) and hp + 1 >= PAIRS)
                    more2 = not (is_last(b) and hp + 2 >= PAIRS)
                    ahead = not (is_last(b) and hp + AHEAD >= PAIRS)
                    older = not (is_first(b) and hp == 0)
                    scores(b, hp, 0)
                    scores(b, hp, 1)
                    if more1:
                        max_transpose(*next_pair(b, hp, 1), j + AHEAD if ahead else B * PAIRS)
                    if ahead:
                        k_project(*next_pair(b, hp, AHEAD))
                    if more2:
                        max_scores(*next_pair(b, hp, 2), 0)
                    if ahead:
                        q_project(*next_pair(b, hp, AHEAD))
                    if older:
                        values(*back(b, hp, 1), 0)
                    if ot_group(b, hp):
                        o_transposes(*ot_group(b, hp))
                    if hp == PROJECT_STEP and not is_first(b):
                        project(b - 1)
                    if hp == CTX_STEP:
                        v_project(*v_group(b, hp))
                    scores(b, hp, 2)
                    if older:
                        values(*back(b, hp, 1), 1)
                    scores(b, hp, 3)
                    if more2:
                        max_scores(*next_pair(b, hp, 2), 1)
                    if v_group(b, hp) and hp != CTX_STEP:
                        v_project(*v_group(b, hp))
                    if hp == CTX_STEP and not is_last(b):
                        ctx_transposes(b + 1)
                if is_last(b):
                    values(b, PAIRS - 1, 0)
                    values(b, PAIRS - 1, 1)
                    o_transposes(b, 2)
                    o_transposes(b, 3)
                    project(b)

            each_batch(pe, batch)

            for i in range(TT // 4):
                if i >= 2:
                    pe.wait_ge(tokt_done, i - 1)
                for n in range(4):
                    pe.wait_ge(tok_done, 4 * i + n + 1)
                    last = pe.transpose(psS[i % 2][:, P * n:P * n + P], tok[:, 4 * i + n, :], ident[:])
                last.then_inc(tokt_psum, 1)
            pe.wait_ge(tokt_done, TT // 4)
            pe.wait_ge(exp_w_in, 32)
            for t in range(TT):
                last = pe.matmul(psX[:, E * t:E * t + E], tT[:, P * t:P * t + P], gw[:], start=True, stop=True)
            last.then_inc(logit_psum, 1)
            pe.wait_ge(route, 5)
            pe.wait_ge(pool_consts, 3)
            hots = hot_padded[:].rearrange("p t e -> p (t e)")
            pe.matmul(psO[:, 0:TT * E], tri[:], hots[:, TT * E:2 * TT * E], start=True, stop=False)
            for s in range(1, TT):
                last = pe.matmul(psO[:, 0:TT * E], ones_bf[:], hots[:, (TT - s) * E:(2 * TT - s) * E],
                                 start=False, stop=(s == TT - 1))
            last.then_inc(pos_psum, 1)
            pe.wait_ge(xe_in, 16)
            for i in range(3):
                if i == 2:
                    pe.wait_ge(xet_done, 1)
                for n in range(min(4, ST_TILES - 4 * i)):
                    last = pe.transpose(psS[i % 2][:, P * n:P * n + P], xe[:, 4 * i + n, :], ident[:])
                last.then_inc(xet_psum, 1)
            pe.wait_ge(xet_done, 3)
            pe.wait_ge(w2_in, 16)

            def up(e):
                for i in range(2):
                    if e:
                        pe.wait_ge(h_done, 2 * e - 1 + i)
                    for f in (2 * i, 2 * i + 1):
                        last = pe.matmul(psM[:, i, (f % 2) * CAP:(f % 2) * CAP + CAP], w1s[:, e, P * f:P * f + P],
                                         xeT[:, e * CAP:(e + 1) * CAP], start=True, stop=True)
                    last.then_inc(h_psum, 1)

            def down(e):
                pe.wait_ge(h_done, 2 * e + 2)
                if e >= 2:
                    pe.wait_ge(y_done, e - 1)
                for f in range(FT):
                    last = pe.matmul([psO, psX][e % 2][:, 0:CAP], w2s[:, e, f, :], hT[:, e % 2, f, :],
                                     start=(f == 0), stop=(f == FT - 1))
                last.then_inc(y_psum, 1)

            for e in range(E):
                up(e)
                if e:
                    down(e - 1)
            down(E - 1)
            pe.wait_ge(y_done, E)
            for i in range(3):
                if i == 2:
                    pe.wait_ge(yrow_done, 1)
                for n in range(min(4, ST_TILES - 4 * i)):
                    s = 4 * i + n
                    last = pe.transpose(psS[i % 2][:, P * n:P * n + P], yT[:, P * s:P * s + P], ident[:])
                last.then_inc(yrow_psum, 1)


_INS = ['x', 'ctx_1024', 'g_xattn', 'g_ffn', 'L0_xattn_ln_gamma', 'L0_xattn_ln_beta', 'L0_xattn_w_q',
        'L0_xattn_w_kv', 'L0_xattn_w_out', 'L0_xattn_b_out', 'L0_xattn_gate', 'L0_ffn_gate_w',
        'L0_ffn_w1', 'L0_ffn_w2']
_OUTS = [((8, 256, 128), 'float32')]


def kernel(**inputs):
    import numpy as _np
    import concourse.bacc as _bacc
    from concourse import mybir as _mybir
    from concourse.bass_utils import run_bass_kernel_spmd as _run

    nc = _bacc.Bacc("TRN2", target_bir_lowering=False, num_devices=1)
    arrays, args = {}, {}
    for name in _INS:
        a = _np.ascontiguousarray(inputs[name])
        arrays[f"in_{name}_dram"] = a
        args[name] = nc.dram_tensor(f"in_{name}_dram", a.shape, _mybir.dt.from_np(a.dtype), kind="ExternalInput").ap()
    for i, (shape, dtype) in enumerate(_OUTS):
        dt = _mybir.dt.from_np(_np.dtype(dtype))
        out = nc.dram_tensor(f"out_{i}_dram", shape, dt, kind="ExternalOutput").ap()
    gated_block(nc, args['x'], args['ctx_1024'], args['g_xattn'], args['g_ffn'], args['L0_xattn_ln_gamma'],
                args['L0_xattn_ln_beta'], args['L0_xattn_w_q'], args['L0_xattn_w_kv'], args['L0_xattn_w_out'],
                args['L0_xattn_b_out'], args['L0_xattn_gate'], args['L0_ffn_gate_w'], args['L0_ffn_w1'],
                args['L0_ffn_w2'], out)
    r = _run(nc, [arrays], core_ids=[0])
    return r.results[0]["out_0_dram"]
```

```python
from contextlib import ExitStack

import concourse.bass as bass
from concourse import mybir

F32 = mybir.dt.float32
F32R = mybir.dt.float32r
F16 = mybir.dt.float16
BF16 = mybir.dt.bfloat16
U32 = mybir.dt.uint32
ALU = mybir.AluOpType
ACT = mybir.ActivationFunctionType
AX = mybir.AxisListType

P = 128


def gated_block(nc, x, ctx_1024, g_xattn, g_ffn, ln_gamma, ln_beta, w_q, w_kv, w_out, b_out, gate,
                gate_w, w1, w2, out):
    B, SQ, D = x.shape
    SK = ctx_1024.shape[1]
    INNER = w_q.shape[1]
    DH = 64
    H = INNER // DH
    PAIRS = H // 2
    QT = SQ // P
    KT = SK // P
    TT = B * QT
    E, _, F = w1.shape
    FT = F // P
    CAP = 160
    SLOTS = E * CAP
    ST_TILES = SLOTS // P
    SCALE = float(DH) ** -0.5
    EPS = 1e-5
    KQ = SK + SQ
    BQ, BK, AK, AQ = 0, SQ, KQ, KQ + SK
    STW = 2 * KQ
    H_QLO, H_KHI, H_QHI, H_KLO, H_QHI2 = 0, SQ, SQ + SK, 2 * SQ + SK, 2 * KQ
    HLW = 2 * KQ + SQ
    LIFT = 0.875
    AHEAD = 4
    BUFS = AHEAD
    DROPPED = 4096.0

    ROW = 2 * D + 2
    R_X, R_ID, R_PROB = D, 2 * D, 2 * D + 1
    table = nc.dram_tensor("experts_table", (SLOTS, ROW), F32).ap()

    with ExitStack() as ctx:
        def sb(name, shape, dt):
            return ctx.enter_context(nc.sbuf_tensor(name, shape, dt))

        def pb(name, shape, dt=F32):
            return ctx.enter_context(nc.psum_tensor(name, shape, dt))

        def sem(name):
            return ctx.enter_context(nc.semaphore(name))

        ident = sb("ident", [P, P], F32)
        gamma = sb("gamma", [P, 1], F32)
        beta = sb("beta", [P, 1], F32)
        gates = sb("gates", [P, 3], F32)
        tgates = sb("tgates", [P, 3], F32)
        gscale = sb("gscale", [P, 1], F32)
        w_hi = sb("w_hi", [P, 3 * INNER], F32R)
        w_lo = sb("w_lo", [P, 3 * INNER], F32R)
        wo = sb("wo", [P, PAIRS, D], F32)
        bo = sb("bo", [P, D], F32)
        X1 = sb("X1", [P, TT, D], F32)
        ctx_raw = sb("ctx_raw", [P, KT, D], F32)
        cT_hi = sb("cT_hi", [P, SK], F32R)
        cT_lo = sb("cT_lo", [P, SK], F32R)
        HL = sb("HL", [P, 2, HLW], F32R)
        ST = sb("ST", [P, BUFS, 2, STW], F32R)
        VH = sb("VH", [P, KT, H, DH + 2], F16)
        VL = sb("VL", [P, KT, H, DH], F16)
        P32 = sb("P32", [P, 2, KT * SQ], F32)
        PARTS = sb("PARTS", [P, 2, 2, 2, KT * SQ], F16)
        PHI, PLO = PARTS[:, 0], PARTS[:, 1]
        parts32 = PARTS[:].rearrange("p a b h n -> p (a b h n)").bitcast(F32)
        wraw = parts32[:, 0:3 * INNER]
        MX = sb("MX", [P, 2, 2, QT], F32)
        MXS = sb("MXS", [P, 2, QT, 2, 2], F32R)
        MROW = sb("MROW", [4 * QT, 2, P], F32R)
        rden = sb("rden", [P, 2, 2 * QT], F32)
        O = sb("O", [P, QT, INNER], F32)
        OT = sb("OT", [P, QT * PAIRS, P], F32)
        stats = sb("stats", [P, TT, 6], F32)
        mv = sb("mv", [P, TT, 2], F32)
        vv = sb("vv", [P, TT], F32)
        rstd = sb("rstd", [P, TT], F32)
        mhalf = sb("mhalf", [P, TT], F32)
        gw = sb("gw", [P, E], F32)
        row = sb("row", [P, QT, ROW], F32)
        tok, x_now = row[:, :, 0:D], row[:, :, R_X:R_X + D]
        tT = sb("tT", [P, QT * P], F32)
        mark = sb("mark", [P, 1], F32)
        pool_mark = sb("pool_mark", [P, 1], F32)
        lmax = sb("lmax", [P, QT], F32)
        lexp = sb("lexp", [P, QT, E], F32)
        lsum = sb("lsum", [P, QT], F32)
        prob1 = sb("prob1", [P, QT], F32)
        cand = sb("cand", [P, QT, E], F32)
        winners = sb("winners", [P, QT, E], F32)
        iota_e = sb("iota_e", [P, QT, E], F32)
        first = sb("first", [P, QT], F32)
        hot_padded = sb("hot_padded", [P, QT + 3, E], BF16)
        hot = hot_padded[:, 2:2 + QT, :]
        tri = sb("tri", [P, P], BF16)
        ones_bf = sb("ones_bf", [P, P], BF16)
        taken = sb("taken", [P, E], F32)
        rank = sb("rank", [P, QT, E], F32)
        rank_hot = sb("rank_hot", [P, QT, E], F32)
        pos = sb("pos", [P, QT], F32)
        slotf = sb("slotf", [P, QT], F32)
        over = sb("over", [P, QT], F32)
        slot_now = sb("slot_now", [P, QT], U32)
        ids = sb("ids", [P, TT], F32)
        empty = sb("empty", [P, ST_TILES], F32)
        target = sb("target", [P, ST_TILES], U32)
        w1s = sb("w1s", [P, E, F], F32)
        with ExitStack() as early:
            xT_hi = early.enter_context(nc.sbuf_tensor("xT_hi", [P, TT * P], F32R))
            xT_lo = early.enter_context(nc.sbuf_tensor("xT_lo", [P, TT * P], F32R))
        w2s = sb("w2s", [P, E, FT, D], F32)
        p32 = P32[:].rearrange("p h n -> p (h n)")
        xe = parts32[:, 0:ST_TILES * ROW].rearrange("p (t d) -> p t d", d=ROW)
        xeT = O[:].rearrange("p q n -> p (q n)")[:, 0:SLOTS]
        hT = VL[:].rearrange("p k h d -> p (k h d)").bitcast(F32)[:, 0:2 * FT * CAP]\
            .rearrange("p (b f c) -> p b f c", b=2, f=FT)
        yT = VH[:].rearrange("p k h d -> p (k h d)").bitcast(F32)[:, 0:SLOTS]
        yrows = p32[:, 0:SLOTS].rearrange("p (t d) -> p t d", d=D)
        zeros = O[:].rearrange("p q n -> p (q n)")

        ZERO_COLS = SLOTS // 2 // P * ROW

        psS = [pb(f"psS{i}", [P, 512]) for i in range(2)]
        psM = pb("psM", [P, QT, 512])
        psKQ = pb("psKQ", [P, 1024])
        psO = pb("psO", [P, 512])
        psX = pb("psX", [P, 512])
        ps_logits = psO[:, 264:264 + QT * E]
        ps_ranks = psO[:, 288:288 + (QT + 1) * E]

        x_in = sem("x_in")
        x_rest_in = sem("x_rest_in")
        small_in = sem("small_in")
        w_in = [sem(f"w_in{i}") for i in range(6)]
        tgates_in = sem("tgates_in")
        wo_in = sem("wo_in")
        bo_in = sem("bo_in")
        bo_scaled = sem("bo_scaled")
        x_biased = sem("x_biased")
        ctx_in = sem("ctx_in")
        exp_w_in = sem("exp_w_in")
        w2_in = sem("w2_in")
        ident_zero = sem("ident_zero")
        ident_ready = sem("ident_ready")
        pool_consts = sem("pool_consts")
        stack_consts = sem("stack_consts")
        stats_done = sem("stats_done")
        mv_done = sem("mv_done")
        vv_done = sem("vv_done")
        rstd_done = sem("rstd_done")
        xn_done = sem("xn_done")
        xn_rest_done = sem("xn_rest_done")
        w_hi_done = sem("w_hi_done")
        w_lo_done = sem("w_lo_done")
        w_lo_rest_done = sem("w_lo_rest_done")
        xt_psum = sem("xt_psum")
        xt_f32 = sem("xt_f32")
        xt_hi_done = sem("xt_hi_done")
        xt_lo_done = sem("xt_lo_done")
        ctxt_psum = sem("ctxt_psum")
        ctxt_hi_done = sem("ctxt_hi_done")
        ctxt_lo_done = sem("ctxt_lo_done")
        kq_psum = sem("kq_psum")
        kq_hi_done = sem("kq_hi_done")
        kq_lo_done = sem("kq_lo_done")
        stack_in = [sem(f"stack_in{i}") for i in range(BUFS)]
        smax_psum = sem("smax_psum")
        max_done = sem("max_done")
        mt_psum = sem("mt_psum")
        mxs_hi_done = sem("mxs_hi_done")
        mxs_lo_done = sem("mxs_lo_done")
        mrow_done = sem("mrow_done")
        mrow_in = [sem(f"mrow_in{i}") for i in range(2)]
        score_psum = sem("score_psum")
        exp_done = sem("exp_done")
        phi0_done = sem("phi0_done")
        phi1_done = sem("phi1_done")
        plo_done = sem("plo_done")
        v_psum = sem("v_psum")
        v_hi_done = sem("v_hi_done")
        v_lo_done = sem("v_lo_done")
        pv_done = sem("pv_done")
        rden_done = sem("rden_done")
        norm_done = sem("norm_done")
        ot_psum = sem("ot_psum")
        ot_done = sem("ot_done")
        proj_psum = sem("proj_psum")
        x1_done = sem("x1_done")
        tgate_done = sem("tgate_done")
        gscale_done = sem("gscale_done")
        zeros_done = sem("zeros_done")
        tok_done = sem("tok_done")
        tokt_psum = sem("tokt_psum")
        tokt_done = sem("tokt_done")
        logit_psum = sem("logit_psum")
        route = sem("route")
        lexp_done = sem("lexp_done")
        pos_psum = sem("pos_psum")
        slot_done = sem("slot_done")
        scattered = sem("scattered")
        xe_in = [sem(f"xe_in{i}") for i in range(3)]
        xet_psum = sem("xet_psum")
        xet_done = sem("xet_done")
        h_psum = sem("h_psum")
        h_done = sem("h_done")
        y_psum = sem("y_psum")
        y_done = sem("y_done")
        yrow_psum = sem("yrow_psum")
        x1_out = sem("x1_out")
        target_done = sem("target_done")
        final_done = sem("final_done")
        out_done = sem("out_done")

        x_t = x.rearrange("b (t p) d -> p (b t) d", p=P)
        out_b = out.rearrange("b (t p) d -> b p t d", p=P)
        out_rows = out.rearrange("b s d -> (b s) d")
        ctx_t = ctx_1024.rearrange("b (t p) d -> b p t d", p=P)

        def slots(b):
            for hp in range(PAIRS):
                yield b * PAIRS + hp, hp

        def back(b, hp, k):
            return (b, hp - k) if hp >= k else (b - 1, hp - k + PAIRS)

        def is_last(b):
            return isinstance(b, int) and b == B - 1

        def is_first(b):
            return isinstance(b, int) and b == 0

        def each_batch(eng, body):
            body(0)
            with eng.Fori(1, B - 1) as b:
                body(b)
            body(B - 1)

        def stack_value(b, hp):
            return b * (64 * PAIRS // BUFS) + 64 * (hp // BUFS + 1)

        def mrow_value(b, hp):
            return b * (32 * PAIRS // 2) + 32 * (hp // 2 + 1)

        def v_group(b, hp):
            if hp < KT:
                return (b, 1, hp)
            return None if is_last(b) else (b + 1, 0, hp - KT)

        OT_STEPS = {4: (0, 0), 6: (0, 1), 0: (1, 2), 1: (1, 3)}

        def ot_group(b, hp):
            if hp not in OT_STEPS or (is_first(b) and OT_STEPS[hp][0]):
                return (b, 2) if is_last(b) and hp == PAIRS - 1 else None
            return (b - OT_STEPS[hp][0], OT_STEPS[hp][1])


        PROJECT_STEP = 2
        CTX_STEP = KT - 1

        def next_pair(b, hp, k):
            return (b, hp + k) if hp + k < PAIRS else (b + 1, hp + k - PAIRS)

        HALF = INNER // 2
        W_PARTS = [(c, half) for half in range(2) for c in (1, 0, 2)]

        def w_cols(part):
            c, half = W_PARTS[part]
            return slice(c * INNER + half * HALF, c * INNER + (half + 1) * HALF)

        XCHUNKS = [(0, QT)] + [(t, min(t + 4, TT)) for t in range(QT, TT, 4)]
        X_STEPS = {0: 1, 1: 2, 2: 3, 5: 4}
        POOL_TILES = range(*XCHUNKS[1])
        DVE_TILES = [t for t in range(TT) if t not in POOL_TILES]

        def x_bank(i):
            return psX if i else psO

        def x_stage(i):
            n = P * (XCHUNKS[i][1] - XCHUNKS[i][0])
            return O[:, 1, INNER - n:INNER] if i else P32[:, 0, 0:n]

        def kq_banks(j):
            if j in (1, 3):
                return psS[0][:, 0:SK], psS[1][:, 0:SQ]
            return psKQ[:, 0:SK], psKQ[:, SK:KQ]

        V_BANKS = [psX, psO, psX, psO]

        MOMENTS_STEP, TOK_STEP, TOKT_STEP, LOGITS_STEP, RANKS_STEP = 3, 4, 5, 6, 7
        BIAS_STEP = PAIRS - TT // 4
        ROUTE = 16

        OUT_GROUPS = ST_TILES // 2
        ROWS_AFTER = [-(-2 * P * (i + 1) // CAP) - 1 for i in range(OUT_GROUPS)]
        ROWS_BEFORE = [-(-(e + 1) * CAP // (4 * P)) for e in range(E)]
        LATE_ROWS = 3

        block = ctx.enter_context(nc.Block())

        @block.sync
        def _(sp):
            def load_w(part):
                c, half = W_PARTS[part]
                cols = slice(half * HALF, (half + 1) * HALF)
                src = w_q[:, cols] if c == 0 else w_kv[:, (c - 1) * INNER + half * HALF:(c - 1) * INNER + (half + 1) * HALF]
                sp.dma_start(wraw[:, w_cols(part)], src).then_inc(w_in[part], 16)

            sp.dma_start(X1[:, 0:QT, :], x_t[:, 0:QT, :]).then_inc(x_in, 16)
            sp.dma_start(ctx_raw[:], ctx_t[0]).then_inc(ctx_in, 16)
            load_w(0)
            load_w(1)
            sp.dma_start(gamma[:], ln_gamma.rearrange("(p o) -> p o", o=1)).then_inc(small_in, 16)
            sp.dma_start(beta[:], ln_beta.rearrange("(p o) -> p o", o=1)).then_inc(small_in, 16)
            load_w(2)
            sp.dma_start(X1[:, QT:TT, :], x_t[:, QT:TT, :]).then_inc(x_rest_in, 16)
            for part in range(3, 6):
                load_w(part)
            for i, g in enumerate((g_xattn, gate, g_ffn)):
                sp.dma_start(gates[:, i:i + 1], g.rearrange("(o n) -> o n", o=1).to_broadcast([P, 1])).then_inc(tgates_in, 16)
            def stacks(b, hp):
                j = b * PAIRS + hp
                buf, par = hp % BUFS, hp % 2
                sp.wait_ge(kq_lo_done, 2 * j + 2)
                sp.wait_ge(kq_hi_done, 2 * j + 2)
                if not (is_first(b) and hp < BUFS):
                    sp.wait_ge(score_psum, 4 * j - 4 * (BUFS - 1))
                for h in range(2):
                    parts = HL[64 * h:64 * h + 64, par, :].bitcast(F32)
                    both = bass.AP(parts.tensor, parts.offset, [parts.ap[0], [SQ, 2], [1, KQ]])
                    sp.dma_start(ST[0:64, buf, h, :].bitcast(F32).rearrange("p (g n) -> p g n", g=2), both)\
                      .then_inc(stack_in[buf], 16)
                    sp.dma_start(ST[64:128, buf, h, AK:STW].bitcast(F32), parts[:, H_KLO:H_KLO + KQ])\
                      .then_inc(stack_in[buf], 16)

            def max_rows(b, hp):
                j = b * PAIRS + hp
                buf, par = hp % BUFS, hp % 2
                sp.wait_ge(mrow_done, j + 1)
                for qt in range(QT):
                    dst = ST[64:66, buf, :, BQ + P * qt:BQ + P * qt + P].bitcast(F32)
                    sp.dma_start(dst, MROW[4 * qt:4 * qt + 4, par, :].bitcast(F32))\
                      .then_inc(mrow_in[par], 16)

            def x1_store(b):
                sp.wait_ge(x1_done, B - 1 + QT if is_last(b) else b + 1)
                sp.dma_start(out_b[b], x_now).then_inc(x1_out, 16)

            for hp in range(AHEAD - 1):
                stacks(0, hp)
            sp.wait_ge(stack_consts, 1)
            max_rows(0, 0)
            stacks(0, AHEAD - 1)
            sp.dma_start(bo[:], b_out.rearrange("(o n) -> o n", o=1).to_broadcast([P, D])).then_inc(bo_in, 16)
            sp.dma_start(wo[:], w_out.rearrange("(c p) n -> p c n", p=P)).then_inc(wo_in, 16)
            sp.dma_start(gw[:], gate_w).then_inc(exp_w_in, 16)

            def batch(b):
                for j, hp in slots(b):
                    if hp == 0 and not is_last(b):
                        sp.wait_ge(ctxt_psum, b + 1)
                        sp.dma_start(ctx_raw[:], ctx_t[b + 1]).then_inc(ctx_in, 16)
                    if not (is_last(b) and hp + 1 >= PAIRS):
                        max_rows(*next_pair(b, hp, 1))
                    if not (is_last(b) and hp + AHEAD >= PAIRS):
                        stacks(*next_pair(b, hp, AHEAD))
                    if hp == MOMENTS_STEP and not is_first(b):
                        x1_store(b - 1)
                    if is_first(b) and hp % (PAIRS // 4) == 1:
                        for e in (hp - 1, hp):
                            sp.dma_start(w1s[:, e, :], w1[e]).then_inc(exp_w_in, 16)
                    if is_last(b) and hp >= PAIRS - AHEAD:
                        if hp == PAIRS - AHEAD:
                            sp.wait_ge(kq_psum, B * PAIRS)
                        for e in (2 * (hp + AHEAD - PAIRS), 2 * (hp + AHEAD - PAIRS) + 1):
                            sp.dma_start(w2s[:, e], w2[e].rearrange("(c p) d -> p c d", p=P)).then_inc(w2_in, 16)

            each_batch(sp, batch)

            x1_store(B - 1)
            sp.wait_ge(scattered, 32 + 16 * TT)
            for i in range(3):
                tiles = slice(4 * i, min(4 * i + 4, ST_TILES))
                sp.dma_start(xe[:, tiles, :], table.rearrange("(t p) d -> p t d", p=P)[:, tiles, :]).then_inc(xe_in[i], 16)
            sp.wait_ge(x1_out, 16 * B)
            sp.wait_ge(out_done, 16 * ST_TILES)

        @block.gpsimd
        def _(pool):
            pool.memset(ident[:], 0.0).then_inc(ident_zero, 1)
            pool.wait_ge(ident_zero, 1)
            pool.affine_select(out=ident[:], in_=ident[:], compare_op=ALU.not_equal, fill=1.0, base=0,
                               pattern=[[-1, P]], channel_multiplier=1).then_inc(ident_ready, 1)
            pool.memset(mhalf[:], -0.5).then_inc(pool_consts, 1)
            pool.wait_ge(pool_consts, 1)
            pool.memset(ST[:].bitcast(F32)[64:128, :, :, BQ:BK], LIFT).then_inc(stack_consts, 1)
            pool.wait_ge(vv_done, 1)
            pool.wait_ge(stack_consts, 1)
            pool.tensor_tensor(rstd[:, 0:QT], vv[:, 0:QT], mhalf[:, 0:QT], ALU.pow).then_inc(rstd_done, 1)
            pool.wait_ge(rstd_done, 1)
            pool.memset(ST[:].bitcast(F32)[64:128, :, :, BK:AK], 1.0).then_inc(stack_consts, 1)
            pool.wait_ge(stack_consts, 2)
            pool.memset(VH[:, :, :, DH:DH + 2], 1.0).then_inc(stack_consts, 1)
            for part in range(3, 6):
                cs = w_cols(part)
                pool.wait_ge(w_hi_done, part + 1)
                pool.tensor_tensor(w_lo[:, cs], wraw[:, cs], w_hi[:, cs].bitcast(F32), ALU.subtract)\
                    .then_inc(w_lo_rest_done, 1)
            for n, (t0, t1) in enumerate((XCHUNKS[1], (XCHUNKS[1][1], TT))):
                pool.wait_ge(vv_done, n + 2)
                pool.tensor_tensor(rstd[:, t0:t1], vv[:, t0:t1], mhalf[:, t0:t1], ALU.pow).then_inc(rstd_done, 1)
                if n == 0:
                    pool.wait_ge(rstd_done, 2)
                    for t in POOL_TILES:
                        pool.tensor_scalar(OT[:, t, :], X1[:, t, :], mv[:, t, 0:1], rstd[:, t:t + 1], ALU.subtract,
                                           ALU.mult).then_inc(xn_rest_done, 1)
            pool.memset(zeros[:, 0:ZERO_COLS], 0.0).then_inc(zeros_done, 1)
            pool.memset(ones_bf[:], 1.0).then_inc(ident_zero, 1)
            pool.wait_ge(ident_zero, 2)
            pool.affine_select(out=tri[:], in_=ones_bf[:], compare_op=ALU.is_ge, fill=0.0, base=0,
                               pattern=[[1, P]], channel_multiplier=-1).then_inc(pool_consts, 1)
            pool.iota(iota_e[:], pattern=[[0, QT], [1, E]], base=-E, channel_multiplier=0,
                      allow_small_or_imprecise_dtypes=True).then_inc(ident_zero, 1)
            pool.memset(hot_padded[:], 0.0).then_inc(pool_consts, 1)
            pool.memset(taken[:], 0.0).then_inc(pool_consts, 1)
            pool.iota(ids[:], pattern=[[P, TT]], base=1, channel_multiplier=1,
                      allow_small_or_imprecise_dtypes=True).then_inc(ident_zero, 1)
            pool.wait_ge(zeros_done, 1)
            for i in range(2):
                half_rows = slice(i * SLOTS // 2, (i + 1) * SLOTS // 2)
                pool.dma_start(table[half_rows, :].rearrange("(p t) d -> p (t d)", p=P), zeros[:, 0:ZERO_COLS])\
                    .then_inc(scattered, 16)

            def token_rstd(b):
                pool.wait_ge(vv_done, 3 + b + 1)
                pool.tensor_tensor(rstd[:, 0:QT], vv[:, 0:QT], mhalf[:, 0:QT], ALU.pow).then_inc(rstd_done, 1)

            def scatter(b):
                pool.wait_ge(slot_done, b + 1)
                pool.wait_ge(scattered, 32 + b * 16 * QT)
                pool.wait_ge(x1_out, 16 * b + 16)
                pool.tensor_tensor(pool_mark[:], mhalf[:, 0:1], mhalf[:, 0:1], ALU.mult)
                for t in range(QT):
                    pool.indirect_dma_start(out=table, out_offset=bass.IndirectOffsetOnAxis(slot_now[:, t:t + 1], 0),
                                            in_=row[:, t, :], in_offset=None, bounds_check=SLOTS - 1,
                                            oob_is_err=False).then_inc(scattered, 16)

            def batch(b):
                for j, hp in slots(b):
                    for h in range(2):
                        par = hp % 2
                        pool.wait_ge(exp_done, 4 * j + 2 * h + 2)
                        pool.wait_ge(phi0_done if h == 0 else phi1_done, j + 1)
                        if not (is_first(b) and hp < 2):
                            pool.wait_ge(pv_done, 2 * j - 4 + h + 1)
                        pool.tensor_tensor(PLO[:, par, h, :], P32[:, h, :], PHI[:, par, h, :],
                                           ALU.subtract).then_inc(plo_done, 1)
                    if is_first(b) and hp >= BIAS_STEP:
                        pool.wait_ge(bo_scaled, 1)
                        for i in range(4 * (hp - BIAS_STEP), 4 * (hp - BIAS_STEP) + 4, 2):
                            pool.tensor_tensor(X1[:, i:i + 2, :], X1[:, i:i + 2, :],
                                               bo[:].unsqueeze(1).to_broadcast([P, 2, D]), ALU.add).then_inc(x_biased, 1)
                    if hp == MOMENTS_STEP and not is_first(b):
                        token_rstd(b - 1)
                    if hp == RANKS_STEP and not is_first(b):
                        scatter(b - 1)

            each_batch(pool, batch)

            token_rstd(B - 1)
            scatter(B - 1)
            pool.wait_ge(x1_out, 16 * B)
            pool.wait_ge(target_done, 2)
            for t in range(ST_TILES):
                pool.wait_ge(final_done, t + 1)
                pool.indirect_dma_start(out=out_rows, out_offset=bass.IndirectOffsetOnAxis(target[:, t:t + 1], 0),
                                        in_=yrows[:, t, :], in_offset=None, bounds_check=TT * P - 1,
                                        oob_is_err=False).then_inc(out_done, 16)

        @block.scalar
        def _(act):
            def split_w(part):
                cs = w_cols(part)
                act.wait_ge(w_in[part], 16)
                act.activation(w_hi[:, cs], wraw[:, cs], ACT.Copy).then_inc(w_hi_done, 1)

            def xt_hi(i):
                t0, t1 = XCHUNKS[i]
                act.wait_ge(xt_psum, i + 1)
                if i == 0:
                    act.wait_ge(small_in, 32)
                if i:
                    act.wait_ge(xt_lo_done, i)
                act.activation(x_stage(i), x_bank(i)[:, 0:P * (t1 - t0)], ACT.Identity, bias=beta[:, 0:1],
                               scale=gamma[:, 0:1]).then_inc(xt_f32, 1)
                act.wait_ge(xt_f32, i + 1)
                act.activation(xT_hi[:, P * t0:P * t1], x_stage(i), ACT.Copy).then_inc(xt_hi_done, 1)

            def ctxt_hi(b):
                act.wait_ge(ctxt_psum, b + 1)
                act.activation(cT_hi[:], psX[:], ACT.Copy).then_inc(ctxt_hi_done, 1)

            def kq_hi(b, hp):
                j = b * PAIRS + hp
                act.wait_ge(kq_psum, j + 1)
                if not (is_first(b) and hp < 2):
                    pb_, php = back(b, hp, 2)
                    act.wait_ge(stack_in[php % BUFS], stack_value(pb_, php))
                k_psum, q_psum = kq_banks(j) if is_first(b) else kq_banks(0)
                if is_first(b) and hp in (1, 3):
                    act.activation(HL[:, hp % 2, H_KHI:H_KHI + SK], k_psum, ACT.Copy)
                    act.activation(HL[:, hp % 2, H_QHI:H_QHI + SQ], q_psum, ACT.Copy).then_inc(kq_hi_done, 1)
                else:
                    act.activation(HL[:, hp % 2, H_KHI:H_KHI + KQ], psKQ[:, 0:KQ], ACT.Copy).then_inc(kq_hi_done, 1)
                act.activation(HL[:, hp % 2, H_QHI2:H_QHI2 + SQ], q_psum, ACT.Copy).then_inc(kq_hi_done, 1)

            def max_row(b, hp):
                j = b * PAIRS + hp
                act.wait_ge(mt_psum, j + 1)
                if not (is_first(b) and hp < 2):
                    act.wait_ge(mrow_in[hp % 2], mrow_value(*back(b, hp, 2)))
                act.activation(MROW[:, hp % 2, :], psKQ[0:4 * QT, KQ:KQ + P], ACT.Copy).then_inc(mrow_done, 1)

            def v_hi(b, half, kt, bank=psX):
                n = b * 2 * KT + half * KT + kt
                act.wait_ge(v_psum, n + 1)
                act.activation(VH[:, kt, 8 * half:8 * half + 8, 0:DH],
                               bank[:].rearrange("p (h d) -> p h d", d=DH), ACT.Copy).then_inc(v_hi_done, 1)

            def tokt_copy(b, bank=psX):
                act.wait_ge(tokt_psum, b + 1)
                act.activation(tT[:], bank[:, 0:QT * P], ACT.Copy).then_inc(tokt_done, 1)

            def router_exp(b):
                act.wait_ge(route, b * ROUTE + 2)
                act.activation(lexp[:], cand[:], ACT.Exp).then_inc(lexp_done, 1)

            def ot_copy(b, i, bank=psX):
                act.wait_ge(ot_psum, b * 4 + i + 1)
                if i < 2 and not is_first(b):
                    act.wait_ge(proj_psum, b)
                act.activation(OT[:, 4 * i:4 * i + 4, :], bank[:].rearrange("p (t c) -> p t c", c=P),
                               ACT.Copy).then_inc(ot_done, 1)

            def exps(j, c, first_pairs):
                h = c // 2
                act.wait_ge(score_psum, 4 * j + c + 1)
                if not (first_pairs):
                    act.wait_ge(plo_done, 2 * j - 2 + h + 1)
                act.activation(P32[:, h, 512 * (c % 2):512 * (c % 2) + 512], psS[c % 2][:], ACT.Exp,
                               scale=SCALE).then_inc(exp_done, 1)

            split_w(0)
            ctxt_hi(0)
            xt_hi(0)
            split_w(1)
            split_w(2)
            for hp in range(AHEAD):
                kq_hi(0, hp)
                v_hi(0, 0, hp, V_BANKS[hp])
                if hp == 1:
                    for part in range(3, 6):
                        split_w(part)
            max_row(0, 0)
            act.wait_ge(tgates_in, 48)
            act.activation(tgates[:], gates[:], ACT.Tanh).then_inc(tgate_done, 1)
            act.wait_ge(xt_lo_done, 1)
            act.wait_ge(w_lo_rest_done, 3)

            def batch(b):
                for j, hp in slots(b):
                    start = is_first(b) and hp == 0
                    exps(j, 0, start)
                    exps(j, 1, start)
                    if not (is_last(b) and hp + 1 >= PAIRS):
                        max_row(*next_pair(b, hp, 1))
                    if not (is_last(b) and hp + AHEAD >= PAIRS):
                        kq_hi(*next_pair(b, hp, AHEAD))
                    if ot_group(b, hp):
                        ot_copy(*ot_group(b, hp))
                    if is_first(b) and hp in X_STEPS:
                        xt_hi(X_STEPS[hp])
                    if hp == TOKT_STEP and not is_first(b):
                        tokt_copy(b - 1)
                    if hp == CTX_STEP:
                        v_hi(*v_group(b, hp))
                    exps(j, 2, start)
                    exps(j, 3, start)
                    act.wait_ge(exp_done, 4 * j + 4)
                    if not (is_first(b) and hp < 2):
                        act.wait_ge(pv_done, 2 * j - 2)
                    act.activation(PHI[:, hp % 2, 1, :], P32[:, 1, :], ACT.Copy).then_inc(phi1_done, 1)
                    if v_group(b, hp) and hp != CTX_STEP:
                        v_hi(*v_group(b, hp))
                    if hp == CTX_STEP and not is_last(b):
                        ctxt_hi(b + 1)
                    if hp == LOGITS_STEP and not is_first(b):
                        router_exp(b - 1)

            each_batch(act, batch)
            ot_copy(B - 1, 3, psS[0])
            tokt_copy(B - 1, psS[1])
            router_exp(B - 1)

            def rows_in(i):
                n = min(4, ST_TILES - 4 * i)
                act.wait_ge(xet_psum, i + 1)
                act.activation(xeT[:, 512 * i:512 * i + n * P], psS[i % 2][:, 0:n * P], ACT.Copy).then_inc(xet_done, 1)

            rows_in(0)
            rows_in(1)
            for e in range(E):
                if e == LATE_ROWS:
                    rows_in(2)
                for i in range(2):
                    act.wait_ge(h_psum, 2 * e + i + 1)
                    if e >= 2:
                        act.wait_ge(y_psum, e - 1)
                    act.activation(hT[:, e % 2, 2 * i:2 * i + 2, :],
                                   psM[:, i, 0:2 * CAP].rearrange("p (f c) -> p f c", f=2), ACT.Relu).then_inc(h_done, 1)

        @block.vector
        def _(dve):
            stats_count = [0]

            def moments(t0, t1):
                n = stats_count[0]
                for t in range(t0, t1):
                    dve.bn_stats(stats[:, t, :], X1[:, t, :]).then_inc(stats_done, 1)
                for t in range(t0, t1):
                    dve.wait_ge(stats_done, n + t - t0 + 1)
                    dve.bn_aggr(mv[:, t, :], stats[:, t, :]).then_inc(mv_done, 1)
                dve.wait_ge(mv_done, n + t1 - t0)
                stats_count[0] = n + t1 - t0

            def both_variances(t0, t1):
                dve.tensor_scalar(vv[:, t0:t1], mv[:, t0:t1, 1], 1.0 + EPS, EPS * EPS, ALU.mult, ALU.add)\
                   .then_inc(vv_done, 1)

            def split_w(part):
                cs = w_cols(part)
                dve.wait_ge(w_hi_done, part + 1)
                dve.tensor_tensor(w_lo[:, cs], wraw[:, cs], w_hi[:, cs].bitcast(F32), ALU.subtract).then_inc(w_lo_done, 1)

            def xn(i):
                if i >= 2:
                    dve.wait_ge(rstd_done, 3)
                for t in range(*XCHUNKS[i]):
                    dve.tensor_scalar(OT[:, t, :], X1[:, t, :], mv[:, t, 0:1], rstd[:, t:t + 1], ALU.subtract,
                                      ALU.mult).then_inc(xn_done, 1)

            def xt_lo(i):
                t0, t1 = XCHUNKS[i]
                dve.wait_ge(xt_hi_done, i + 1)
                dve.tensor_tensor(xT_lo[:, P * t0:P * t1], x_stage(i), xT_hi[:, P * t0:P * t1].bitcast(F32),
                                  ALU.subtract).then_inc(xt_lo_done, 1)

            def ctxt_lo(b):
                dve.wait_ge(ctxt_hi_done, b + 1)
                dve.tensor_tensor(cT_lo[:], psX[:], cT_hi[:].bitcast(F32), ALU.subtract).then_inc(ctxt_lo_done, 1)

            def kq_lo(b, hp):
                j = b * PAIRS + hp
                dve.wait_ge(kq_hi_done, 2 * j + 2)
                hl = HL[:, hp % 2, :]
                k_psum, q_psum = kq_banks(j) if is_first(b) else kq_banks(0)
                dve.tensor_tensor(hl[:, H_KLO:H_KLO + SK], k_psum,
                                  hl[:, H_KHI:H_KHI + SK].bitcast(F32), ALU.subtract).then_inc(kq_lo_done, 1)
                dve.tensor_tensor(hl[:, H_QLO:H_QLO + SQ], q_psum,
                                  hl[:, H_QHI:H_QHI + SQ].bitcast(F32), ALU.subtract).then_inc(kq_lo_done, 1)

            def v_lo(b, half, kt, bank=psX):
                n = b * 2 * KT + half * KT + kt
                dve.wait_ge(v_hi_done, n + 1)
                dve.tensor_tensor(VL[:, kt, 8 * half:8 * half + 8, :], bank[:].rearrange("p (h d) -> p h d", d=DH),
                                  VH[:, kt, 8 * half:8 * half + 8, 0:DH], ALU.subtract).then_inc(v_lo_done, 1)

            def row_max(b, hp, h):
                j = b * PAIRS + hp
                dve.wait_ge(smax_psum, 2 * j + h + 1)
                if not (is_first(b) and hp < 2):
                    dve.wait_ge(mt_psum, j - 1)
                dve.tensor_reduce(MX[:, hp % 2, h, :], psM[:], AX.X, ALU.max).then_inc(max_done, 1)

            def split_max(b, hp):
                j = b * PAIRS + hp
                maxima = MX[:, hp % 2].rearrange("p h q -> p q h")
                hi, lo = MXS[:, hp % 2, :, 0, :], MXS[:, hp % 2, :, 1, :]
                dve.wait_ge(max_done, 2 * j + 2)
                dve.tensor_scalar(hi, maxima, -1.0, None, ALU.mult).then_inc(mxs_hi_done, 1)
                dve.wait_ge(mxs_hi_done, j + 1)
                dve.scalar_tensor_tensor(out=lo, in0=maxima, scalar=-1.0, in1=hi.bitcast(F32), op0=ALU.mult,
                                         op1=ALU.subtract).then_inc(mxs_lo_done, 1)

            def normalise_heads(b, hp, start_of_all):
                j = b * PAIRS + hp
                sums = psO[:, 0:2 * QT * (DH + 1)].rearrange("p (g d) -> p g d", d=DH + 1)
                dve.wait_ge(pv_done, 2 * j + 2)
                dve.reciprocal(rden[:, hp % 2, :], sums[:, :, DH]).then_inc(rden_done, 1)
                dve.wait_ge(rden_done, j + 1)
                if hp % 2 == 0 and not is_first(b):
                    dve.wait_ge(ot_psum, b * 4 - 4 + hp // 2 + 1)
                if start_of_all:
                    dve.wait_ge(scattered, 32)
                o = O[:, :, P * hp:P * hp + P].rearrange("p q (h d) -> p h q d", h=2)
                dve.tensor_tensor(o, sums[:, :, 0:DH].rearrange("p (h q) d -> p h q d", h=2),
                                  rden[:, hp % 2, :].rearrange("p (h q) -> p h q", h=2).unsqueeze(3)
                                  .to_broadcast([P, 2, QT, DH]), ALU.mult).then_inc(norm_done, 1)

            def add_attention(b, banks=None):
                dve.wait_ge(proj_psum, b + 1)
                dve.wait_ge(x_biased, TT // 2)
                dve.wait_ge(scattered, 32 + b * 16 * QT)
                if banks:
                    for q, bank in enumerate(banks):
                        dve.scalar_tensor_tensor(out=x_now[:, q, :], in0=bank[:, 0:D], scalar=gscale[:, 0:1],
                                                 in1=X1[:, b * QT + q, :], op0=ALU.mult, op1=ALU.add).then_inc(x1_done, 1)
                    return
                dve.scalar_tensor_tensor(out=x_now, in0=psX[:, 0:QT * D].rearrange("p (q d) -> p q d", q=QT),
                                         scalar=gscale[:, 0:1], in1=X1[:, bass.ds(b * QT, QT), :], op0=ALU.mult,
                                         op1=ALU.add).then_inc(x1_done, 1)

            def token_moments(b):
                dve.wait_ge(x1_done, B - 1 + QT if is_last(b) else b + 1)
                dve.tensor_copy(mark[:], gscale[:])
                for q in range(QT):
                    dve.bn_stats(stats[:, q, :], x_now[:, q, :]).then_inc(stats_done, 1)
                dve.wait_ge(stats_done, TT + b * QT + QT)
                dve.tensor_copy(mark[:], gscale[:])
                for q in range(QT):
                    dve.bn_aggr(mv[:, q, :], stats[:, q, :]).then_inc(mv_done, 1)
                dve.wait_ge(mv_done, TT + b * QT + QT)
                dve.tensor_scalar(vv[:, 0:QT], mv[:, 0:QT, 1], EPS, None, ALU.add).then_inc(vv_done, 1)

            def tokens(b):
                dve.wait_ge(rstd_done, 3 + b + 1)
                for q in range(QT):
                    dve.tensor_scalar(tok[:, q, :], x_now[:, q, :], mv[:, q, 0:1], rstd[:, q:q + 1], ALU.subtract,
                                      ALU.mult).then_inc(tok_done, 1)

            def wide(a):
                return a.unsqueeze(2).to_broadcast([P, QT, E])

            def choose(b):
                n = b * ROUTE
                lg = ps_logits.rearrange("p (t e) -> p t e", e=E)
                dve.wait_ge(logit_psum, b + 1)
                dve.tensor_reduce(lmax[:], lg, AX.X, ALU.max).then_inc(route, 1)
                dve.wait_ge(route, n + 1)
                dve.tensor_tensor(cand[:], lg, wide(lmax[:]), ALU.subtract).then_inc(route, 1)
                dve.wait_ge(route, n + 2)
                dve.scalar_tensor_tensor(out=winners[:], in0=cand[:], scalar=0.0, in1=iota_e[:], op0=ALU.is_equal,
                                         op1=ALU.mult).then_inc(route, 1)
                dve.wait_ge(route, n + 3)
                dve.tensor_reduce(first[:], winners[:], AX.X, ALU.min).then_inc(route, 1)
                dve.wait_ge(route, n + 4)
                dve.tensor_tensor(hot, iota_e[:], wide(first[:]), ALU.is_equal).then_inc(route, 1)

            def place(b):
                n = b * ROUTE
                ranks = ps_ranks.rearrange("p (t e) -> p t e", e=E)
                dve.wait_ge(pos_psum, b + 1)
                dve.tensor_tensor(rank[:], ranks[:, 0:QT, :], taken[:].unsqueeze(1).to_broadcast([P, QT, E]), ALU.add)\
                   .then_inc(route, 1)
                dve.wait_ge(route, n + 6)
                dve.tensor_tensor(taken[:], ranks[:, QT, :], taken[:], ALU.add).then_inc(route, 1)
                dve.tensor_tensor(rank_hot[:], rank[:], hot, ALU.mult).then_inc(route, 1)
                dve.wait_ge(lexp_done, b + 1)
                dve.tensor_reduce(lsum[:], lexp[:], AX.X, ALU.add).then_inc(route, 1)
                dve.wait_ge(route, n + 8)
                dve.tensor_reduce(pos[:], rank_hot[:], AX.X, ALU.add).then_inc(route, 1)
                dve.tensor_scalar(slotf[:], first[:], float(CAP), float(E * CAP - 1), ALU.mult, ALU.add).then_inc(route, 1)
                dve.wait_ge(route, n + 9)
                dve.reciprocal(prob1[:], lsum[:]).then_inc(route, 1)
                dve.wait_ge(route, n + 11)
                dve.tensor_scalar(over[:], pos[:], float(CAP), DROPPED, ALU.is_gt, ALU.mult).then_inc(route, 1)
                dve.tensor_tensor(pos[:], slotf[:], pos[:], ALU.add).then_inc(route, 1)
                dve.wait_ge(route, n + 12)
                dve.tensor_scalar(row[:, :, R_PROB], prob1[:], tgates[:, 2:3], None, ALU.mult).then_inc(route, 1)
                dve.tensor_copy(row[:, :, R_ID], ids[:, bass.ds(b * QT, QT)]).then_inc(route, 1)
                dve.wait_ge(route, n + 16)
                dve.tensor_tensor(slot_now[:], pos[:], over[:], ALU.add).then_inc(slot_done, 1)

            dve.wait_ge(x_in, 16)
            moments(0, QT)
            both_variances(0, QT)
            split_w(0)
            dve.wait_ge(rstd_done, 1)
            xn(0)
            ctxt_lo(0)
            xt_lo(0)
            split_w(1)
            split_w(2)
            for hp in range(2):
                kq_lo(0, hp)
                v_lo(0, 0, hp, V_BANKS[hp])
            dve.wait_ge(x_rest_in, 16)
            moments(*XCHUNKS[1])
            both_variances(*XCHUNKS[1])
            row_max(0, 0, 0)
            kq_lo(0, 2)
            row_max(0, 0, 1)
            split_max(0, 0)
            v_lo(0, 0, 2, V_BANKS[2])
            kq_lo(0, 3)
            v_lo(0, 0, 3, V_BANKS[3])
            row_max(0, 1, 0)
            moments(XCHUNKS[1][1], TT)
            both_variances(XCHUNKS[1][1], TT)
            row_max(0, 1, 1)
            split_max(0, 1)
            dve.wait_ge(tgate_done, 1)
            dve.tensor_tensor(gscale[:], tgates[:, 0:1], tgates[:, 1:2], ALU.mult).then_inc(gscale_done, 1)
            dve.wait_ge(gscale_done, 1)
            dve.wait_ge(ident_zero, 4)
            dve.wait_ge(w_lo_rest_done, 3)

            def batch(b):
                for j, hp in slots(b):
                    more2 = not (is_last(b) and hp + 2 >= PAIRS)
                    dve.wait_ge(exp_done, 4 * j + 2)
                    if not (is_first(b) and hp < 2):
                        dve.wait_ge(pv_done, 2 * j - 3)
                    dve.tensor_copy(PHI[:, hp % 2, 0, :], P32[:, 0, :]).then_inc(phi0_done, 1)
                    if more2:
                        row_max(*next_pair(b, hp, 2), 0)
                    if not (is_last(b) and hp + AHEAD >= PAIRS):
                        kq_lo(*next_pair(b, hp, AHEAD))
                    if is_first(b) and hp in X_STEPS:
                        xt_lo(X_STEPS[hp])
                    if is_first(b) and 0 <= hp < 3:
                        xn(hp + 2)
                    if hp == PROJECT_STEP and not is_first(b):
                        add_attention(b - 1)
                    if hp == CTX_STEP:
                        v_lo(*v_group(b, hp))
                    if hp == LOGITS_STEP and not is_first(b):
                        dve.wait_ge(logit_psum, b)
                    if hp == RANKS_STEP and not is_first(b):
                        dve.wait_ge(pos_psum, b)
                    if not (is_first(b) and hp == 0):
                        normalise_heads(*back(b, hp, 1), is_first(b) and hp == 1)
                    if hp == LOGITS_STEP and not is_first(b):
                        choose(b - 1)
                    if hp == RANKS_STEP and not is_first(b):
                        place(b - 1)
                    if more2:
                        row_max(*next_pair(b, hp, 2), 1)
                        split_max(*next_pair(b, hp, 2))
                    if v_group(b, hp) and hp != CTX_STEP:
                        v_lo(*v_group(b, hp))
                    if hp == CTX_STEP and not is_last(b):
                        ctxt_lo(b + 1)
                    if is_first(b) and hp == BIAS_STEP - 1:
                        dve.wait_ge(bo_in, 16)
                        dve.tensor_scalar(bo[:], bo[:], gscale[:, 0:1], None, ALU.mult).then_inc(bo_scaled, 1)
                    if hp == MOMENTS_STEP and not is_first(b):
                        token_moments(b - 1)
                    if hp == TOK_STEP and not is_first(b):
                        tokens(b - 1)

            each_batch(dve, batch)
            normalise_heads(B - 1, PAIRS - 1, False)
            add_attention(B - 1, [psX, psM[:, 0]])
            token_moments(B - 1)
            tokens(B - 1)
            choose(B - 1)
            place(B - 1)

            for i in range(3):
                dve.wait_ge(xe_in[i], 16)
            dve.tensor_scalar(empty[:], xe[:, :, R_ID], 0.0, DROPPED, ALU.is_equal, ALU.mult).then_inc(target_done, 1)
            dve.wait_ge(target_done, 1)
            dve.scalar_tensor_tensor(out=target[:], in0=xe[:, :, R_ID], scalar=-1.0, in1=empty[:], op0=ALU.add,
                                     op1=ALU.add).then_inc(target_done, 1)

            def y_rows(i):
                dve.wait_ge(yrow_psum, i + 1)
                for n in range(2):
                    t = 2 * i + n
                    dve.scalar_tensor_tensor(out=yrows[:, t, :], in0=psS[i % 2][:, P * n:P * n + P],
                                             scalar=xe[:, t, R_PROB:R_PROB + 1], in1=xe[:, t, R_X:R_X + D],
                                             op0=ALU.mult, op1=ALU.add).then_inc(final_done, 1)

            for e in range(E):
                dve.wait_ge(y_psum, e + 1)
                dve.tensor_copy(yT[:, e * CAP:(e + 1) * CAP], [psO, psX][e % 2][:, 0:CAP]).then_inc(y_done, 1)
                for i in range(OUT_GROUPS):
                    if ROWS_AFTER[i] == e:
                        y_rows(i)
        @block.tensor
        def _(pe):
            def matmul3(dst, hi_l, lo_l, hi_r, lo_r):
                pe.matmul(dst, hi_l, hi_r, start=True, stop=False)
                pe.matmul(dst, hi_l, lo_r, start=False, stop=False)
                return pe.matmul(dst, lo_l, hi_r, start=False, stop=True)

            x_free = [None]

            def wait_x(free_when):
                if x_free[0]:
                    pe.wait_ge(*x_free[0])
                x_free[0] = free_when

            def ctx_transposes(b):
                pe.wait_ge(ctx_in, 16 * b + 16)
                wait_x((ctxt_lo_done, b + 1))
                for kt in range(KT):
                    last = pe.transpose(psX[:, P * kt:P * kt + P], ctx_raw[:, kt, :], ident[:])
                last.then_inc(ctxt_psum, 1)

            def k_project(b, hp):
                j = b * PAIRS + hp
                if not (is_first(b) and hp < 2):
                    pe.wait_ge(kq_lo_done, 2 * j - 2 if is_first(b) and hp < AHEAD else 2 * j)
                if hp == 0:
                    pe.wait_ge(ctxt_lo_done, b + 1)
                k_cols = slice(INNER + P * hp, INNER + P * hp + P)
                k_psum, _ = kq_banks(j) if is_first(b) else kq_banks(0)
                matmul3(k_psum, w_hi[:, k_cols], w_lo[:, k_cols], cT_hi[:], cT_lo[:])

            def q_project(b, hp):
                if not (is_first(b) and hp < AHEAD):
                    pe.wait_ge(mrow_done, b * PAIRS + hp - AHEAD + 2)
                q_cols = slice(P * hp, P * hp + P)
                xs = bass.ds(b * SQ, SQ)
                if not is_first(b) and hp == 0:
                    pe.wait_ge(xt_lo_done, len(XCHUNKS) if not isinstance(b, int) or b > 1 else 2)
                _, q_psum = kq_banks(b * PAIRS + hp) if is_first(b) else kq_banks(0)
                matmul3(q_psum, w_hi[:, q_cols], w_lo[:, q_cols], xT_hi[:, xs], xT_lo[:, xs])\
                    .then_inc(kq_psum, 1)

            def v_project(b, half, kt, bank=psX):
                if bank is psX:
                    wait_x((v_lo_done, b * 2 * KT + half * KT + kt + 1))
                pe.wait_ge(ctxt_lo_done, b + 1)
                cs = slice(P * kt, P * kt + P)
                ws = slice(2 * INNER + 512 * half, 2 * INNER + 512 * half + 512)
                matmul3(bank[:], cT_hi[:, cs], cT_lo[:, cs], w_hi[:, ws], w_lo[:, ws]).then_inc(v_psum, 1)

            def max_scores(b, hp, h):
                j = b * PAIRS + hp
                buf = hp % BUFS
                if h == 0:
                    pe.wait_ge(stack_in[buf], stack_value(b, hp))
                if not (is_first(b) and hp == 0 and h == 0):
                    pe.wait_ge(max_done, 2 * j + h)
                for qt in range(QT):
                    last = pe.matmul(psM[:, qt, :], ST[:, buf, h, AQ + P * qt:AQ + P * qt + P],
                                     ST[:, buf, h, AK:AQ], start=True, stop=True)
                last.then_inc(smax_psum, 1)

            def max_transpose(b, hp, kq_before):
                j = b * PAIRS + hp
                pe.wait_ge(mxs_lo_done, j + 1)
                pe.wait_ge(kq_lo_done, 2 * kq_before)
                maxima = MXS[:, hp % 2].bitcast(F32).rearrange("p q r h -> p (q r h)")
                pe.transpose(psKQ[0:4 * QT, KQ:KQ + P], maxima, ident[:]).then_inc(mt_psum, 1)

            def scores(b, hp, c):
                j = b * PAIRS + hp
                buf, h = hp % BUFS, c // 2
                if c == 0:
                    pe.wait_ge(mrow_in[hp % 2], mrow_value(b, hp))
                if not (is_first(b) and hp == 0 and c < 2):
                    pe.wait_ge(exp_done, 4 * j + c - 1)
                for i in range(2):
                    kt = 2 * (c % 2) + i
                    dst = psS[c % 2][:, SQ * i:SQ * i + SQ]
                    pe.matmul(dst, ST[:, buf, h, AK + P * kt:AK + P * kt + P], ST[:, buf, h, AQ:STW], start=True, stop=False)
                    last = pe.matmul(dst, ST[:, buf, h, BK + P * kt:BK + P * kt + P], ST[:, buf, h, BQ:BK],
                                     start=False, stop=True)
                last.then_inc(score_psum, 1)

            def values(b, hp, h):
                j = b * PAIRS + hp
                par, head = hp % 2, 2 * hp + h
                pe.wait_ge(plo_done, 2 * j + h + 1)
                if h == 0:
                    if not (is_first(b) and hp == 0):
                        pe.wait_ge(norm_done, j)
                    if hp % 4 == 0:
                        pe.wait_ge(v_lo_done, b * 2 * KT + KT * (hp // 4 + 1))
                for qt in range(QT):
                    g = (h * QT + qt) * (DH + 1)
                    for kt in range(KT):
                        cs = slice(SQ * kt + P * qt, SQ * kt + P * qt + P)
                        phi, plo = PHI[:, par, h, cs], PLO[:, par, h, cs]
                        first_, last_ = kt == 0, kt == KT - 1
                        pe.matmul(psO[:, g:g + DH + 1], phi, VH[:, kt, head, 0:DH + 1], start=first_, stop=False)
                        pe.matmul(psO[:, g:g + DH], phi, VL[:, kt, head, :], start=False, stop=False)
                        last = pe.matmul(psO[:, g:g + DH + 1], plo, VH[:, kt, head, 0:DH + 1], start=False,
                                         stop=last_)
                last.then_inc(pv_done, 1)

            def o_transposes(b, i, bank=psX):
                if bank is psX:
                    wait_x((ot_done, b * 4 + i + 1))
                pe.wait_ge(norm_done, b * PAIRS + 2 * i + 2)
                for n in range(4):
                    pair, qt = divmod(4 * i + n, QT)
                    last = pe.transpose(bank[:, P * n:P * n + P], O[:, qt, P * pair:P * pair + P], ident[:])
                last.then_inc(ot_psum, 1)

            def tok_transposes(b, bank=psX):
                if bank is psX:
                    wait_x((tokt_done, b + 1))
                pe.wait_ge(tok_done, b * QT + QT)
                for q in range(QT):
                    last = pe.transpose(bank[:, P * q:P * q + P], tok[:, q, :], ident[:])
                last.then_inc(tokt_psum, 1)

            def logits(b):
                pe.wait_ge(tokt_done, b + 1)
                pe.wait_ge(exp_w_in, 16 + 16 * E)
                for q in range(QT):
                    last = pe.matmul(ps_logits[:, E * q:E * q + E], tT[:, P * q:P * q + P], gw[:], start=True, stop=True)
                last.then_inc(logit_psum, 1)

            def ranks(b):
                pe.wait_ge(route, b * ROUTE + 5)
                for i, (counts, c) in enumerate(((tri, 2), (ones_bf, 1), (ones_bf, 0))):
                    last = pe.matmul(ps_ranks, counts[:], hot_padded[:, c:c + QT + 1, :].rearrange("p t e -> p (t e)"),
                                     start=(i == 0), stop=(i == 2))
                last.then_inc(pos_psum, 1)

            def project_last(b, pairs):
                if not pairs[0]:
                    pe.wait_ge(*x_free[0])
                pe.wait_ge(ot_done, b * 4 + (pairs[-1] + 1) // 2)
                for qt in range(QT):
                    dst = [psX, psM[:, 0]][qt][:, 0:D]
                    for pair in pairs:
                        last = pe.matmul(dst, OT[:, pair * QT + qt, :], wo[:, pair, :], start=(pair == 0),
                                         stop=(pair == PAIRS - 1))
                if pairs[-1] == PAIRS - 1:
                    last.then_inc(proj_psum, 1)

            def project(b):
                wait_x((x1_done, b + 1))
                pe.wait_ge(ot_done, b * 4 + 4)
                pe.wait_ge(wo_in, 16)
                for qt in range(QT):
                    dst = psX[:, D * qt:D * qt + D]
                    for pair in range(PAIRS):
                        last = pe.matmul(dst, OT[:, pair * QT + qt, :], wo[:, pair, :], start=(pair == 0),
                                         stop=(pair == PAIRS - 1))
                last.then_inc(proj_psum, 1)

            pe.wait_ge(ident_ready, 1)
            def x_transposes(i):
                if i:
                    wait_x((xt_f32, i + 1))
                t0, t1 = XCHUNKS[i]
                for t in range(t0, t1):
                    if t in POOL_TILES:
                        pe.wait_ge(xn_rest_done, POOL_TILES.index(t) + 1)
                    else:
                        pe.wait_ge(xn_done, DVE_TILES.index(t) + 1)
                    last = pe.transpose(x_bank(i)[:, P * (t - t0):P * (t - t0) + P], OT[:, t, :], ident[:])
                last.then_inc(xt_psum, 1)

            ctx_transposes(0)
            x_transposes(0)
            pe.wait_ge(w_lo_done, 1)
            k_project(0, 0)
            pe.wait_ge(xt_lo_done, 1)
            pe.wait_ge(w_lo_done, 2)
            q_project(0, 0)
            k_project(0, 1)
            q_project(0, 1)
            pe.wait_ge(w_lo_done, 3)
            v_project(0, 0, 0)
            pe.wait_ge(xt_f32, 1)
            v_project(0, 0, 1, psO)
            k_project(0, 2)
            q_project(0, 2)
            v_project(0, 0, 2)
            pe.wait_ge(stack_consts, 3)
            max_scores(0, 0, 0)
            k_project(0, 3)
            q_project(0, 3)
            pe.wait_ge(v_lo_done, 2)
            v_project(0, 0, 3, psO)
            max_scores(0, 0, 1)
            max_transpose(0, 0, AHEAD - 1)
            max_scores(0, 1, 0)
            max_scores(0, 1, 1)
            pe.wait_ge(kq_lo_done, 2 * AHEAD)
            pe.wait_ge(w_lo_rest_done, 3)

            def batch(b):
                if not is_first(b):
                    x_free[0] = (v_lo_done, b * 2 * KT + KT)
                for j, hp in slots(b):
                    more1 = not (is_last(b) and hp + 1 >= PAIRS)
                    more2 = not (is_last(b) and hp + 2 >= PAIRS)
                    ahead = not (is_last(b) and hp + AHEAD >= PAIRS)
                    older = not (is_first(b) and hp == 0)
                    scores(b, hp, 0)
                    scores(b, hp, 1)
                    if older:
                        values(*back(b, hp, 1), 0)
                    if more1:
                        max_transpose(*next_pair(b, hp, 1), j + AHEAD if ahead else B * PAIRS)
                    if ahead:
                        k_project(*next_pair(b, hp, AHEAD))
                    if more2:
                        max_scores(*next_pair(b, hp, 2), 0)
                    if ahead:
                        q_project(*next_pair(b, hp, AHEAD))
                    if ot_group(b, hp):
                        o_transposes(*ot_group(b, hp))
                    if is_first(b) and hp in X_STEPS:
                        x_transposes(X_STEPS[hp])
                    if hp == PROJECT_STEP and not is_first(b):
                        project(b - 1)
                    if hp == TOKT_STEP and not is_first(b):
                        tok_transposes(b - 1)
                    if hp == CTX_STEP:
                        v_project(*v_group(b, hp))
                    scores(b, hp, 2)
                    if older:
                        values(*back(b, hp, 1), 1)
                    if hp == LOGITS_STEP and not is_first(b):
                        logits(b - 1)
                    if hp == RANKS_STEP and not is_first(b):
                        ranks(b - 1)
                    scores(b, hp, 3)
                    if more2:
                        max_scores(*next_pair(b, hp, 2), 1)
                    if v_group(b, hp) and hp != CTX_STEP:
                        v_project(*v_group(b, hp))
                    if hp == CTX_STEP and not is_last(b):
                        ctx_transposes(b + 1)
                    if hp == LOGITS_STEP and not is_first(b):
                        pe.wait_ge(route, b * ROUTE - ROUTE + 2)
                    if hp == RANKS_STEP and not is_first(b):
                        pe.wait_ge(route, b * ROUTE - ROUTE + 7)
                if is_last(b):
                    project_last(b, range(PAIRS - 2))
                    values(b, PAIRS - 1, 0)
                    values(b, PAIRS - 1, 1)
                    o_transposes(b, 3, psS[0])
                    project_last(b, range(PAIRS - 2, PAIRS))
                    tok_transposes(b, psS[1])
                    logits(b)
                    ranks(b)

            each_batch(pe, batch)

            pe.wait_ge(w2_in, 16 * E)

            def rows_in(i):
                pe.wait_ge(xe_in[i], 16)
                if i == 2:
                    pe.wait_ge(xet_done, 1)
                for n in range(min(4, ST_TILES - 4 * i)):
                    last = pe.transpose(psS[i % 2][:, P * n:P * n + P], xe[:, 4 * i + n, 0:D], ident[:])
                last.then_inc(xet_psum, 1)

            def rows_out(i):
                pe.wait_ge(y_done, ROWS_AFTER[i] + 1)
                pe.wait_ge(xet_done, 3)
                if i >= 2:
                    pe.wait_ge(final_done, 2 * (i - 1))
                for n in range(2):
                    s = 2 * i + n
                    last = pe.transpose(psS[i % 2][:, P * n:P * n + P], yT[:, P * s:P * s + P], ident[:])
                last.then_inc(yrow_psum, 1)

            def up(e):
                for i in range(2):
                    if e:
                        pe.wait_ge(h_done, 2 * e - 1 + i)
                    for f in (2 * i, 2 * i + 1):
                        last = pe.matmul(psM[:, i, (f % 2) * CAP:(f % 2) * CAP + CAP], w1s[:, e, P * f:P * f + P],
                                         xeT[:, e * CAP:(e + 1) * CAP], start=True, stop=True)
                    last.then_inc(h_psum, 1)

            def down(e):
                pe.wait_ge(h_done, 2 * e + 2)
                if e >= 2:
                    pe.wait_ge(y_done, e - 1)
                for f in range(FT):
                    last = pe.matmul([psO, psX][e % 2][:, 0:CAP], w2s[:, e, f, :], hT[:, e % 2, f, :],
                                     start=(f == 0), stop=(f == FT - 1))
                last.then_inc(y_psum, 1)

            rows_in(0)
            rows_in(1)
            for e in range(E):
                if e == LATE_ROWS:
                    rows_in(2)
                pe.wait_ge(xet_done, ROWS_BEFORE[e])
                up(e)
                if e:
                    down(e - 1)
                for i in range(OUT_GROUPS - 1):
                    if ROWS_AFTER[i] == e - 2:
                        rows_out(i)
                    if ROWS_AFTER[i] == e - 1 and e == E - 1:
                        rows_out(i)
            down(E - 1)
            rows_out(OUT_GROUPS - 1)


_INS = ['x', 'ctx_1024', 'g_xattn', 'g_ffn', 'L0_xattn_ln_gamma', 'L0_xattn_ln_beta', 'L0_xattn_w_q',
        'L0_xattn_w_kv', 'L0_xattn_w_out', 'L0_xattn_b_out', 'L0_xattn_gate', 'L0_ffn_gate_w',
        'L0_ffn_w1', 'L0_ffn_w2']
_OUTS = [((8, 256, 128), 'float32')]


def kernel(**inputs):
    import numpy as _np
    import concourse.bacc as _bacc
    from concourse import mybir as _mybir
    from concourse.bass_utils import run_bass_kernel_spmd as _run

    nc = _bacc.Bacc("TRN2", target_bir_lowering=False, num_devices=1)
    arrays, args = {}, {}
    for name in _INS:
        a = _np.ascontiguousarray(inputs[name])
        arrays[f"in_{name}_dram"] = a
        args[name] = nc.dram_tensor(f"in_{name}_dram", a.shape, _mybir.dt.from_np(a.dtype), kind="ExternalInput").ap()
    for i, (shape, dtype) in enumerate(_OUTS):
        dt = _mybir.dt.from_np(_np.dtype(dtype))
        out = nc.dram_tensor(f"out_{i}_dram", shape, dt, kind="ExternalOutput").ap()
    gated_block(nc, args['x'], args['ctx_1024'], args['g_xattn'], args['g_ffn'], args['L0_xattn_ln_gamma'],
                args['L0_xattn_ln_beta'], args['L0_xattn_w_q'], args['L0_xattn_w_kv'], args['L0_xattn_w_out'],
                args['L0_xattn_b_out'], args['L0_xattn_gate'], args['L0_ffn_gate_w'], args['L0_ffn_w1'],
                args['L0_ffn_w2'], out)
    r = _run(nc, [arrays], core_ids=[0])
    return r.results[0]["out_0_dram"]
```
